# Optimizing a Trainium2 kernel written in Bass

```python
import numpy as np
import jax
import jax.numpy as jnp

def _softmax(x, axis=-1):
    return jax.nn.softmax(x, axis=axis)

def _gelu(x):
    return jax.nn.gelu(x, approximate=True)

def _silu(x):
    return jax.nn.silu(x)

def _sigmoid(x):
    return jax.nn.sigmoid(x)

def _layernorm(x, axis=-1, eps=1e-05):
    m = jnp.mean(x, axis=axis, keepdims=True)
    v = jnp.var(x, axis=axis, keepdims=True)
    return (x - m) / jnp.sqrt(v + eps)

def _scatter_add(tgt, idx, src, axis=0):
    return tgt.at[idx].add(src)

def _segment_sum(src, seg, n):
    return jax.ops.segment_sum(src, seg, n)
kernel_name = 'mk_flamingo_gated_d2_seqx_r8_2fed6c'

def setup_inputs(seed: int=0):
    np.random.seed(seed)
    _w = jnp.asarray

    def _rec_inputs():
        import jax
        import jax.numpy as jnp
        _rk = jax.random.key(seed)
        x = 0.0003765 + 1 * jax.random.normal(jax.random.fold_in(_rk, 1), (8, 128, 256), jnp.float32)
        _lenS = 128 - jax.random.randint(jax.random.fold_in(_rk, 7), (8,), 0, max(1, 128 // 4) + 1, jnp.int32)
        _lenS2 = 128 - jax.random.randint(jax.random.fold_in(_rk, 8), (8,), 0, max(1, 128 // 4) + 1, jnp.int32)
        _ctx_2048P = jax.random.normal(jax.random.fold_in(_rk, 11), (8, 16, 256), jnp.float32)
        _ctx_2048c = jax.random.dirichlet(jax.random.fold_in(_rk, 511), 0.3 * jnp.ones((16,), jnp.float32), (8, 128))
        _ctx_2048t = jnp.einsum('bsk,bkd->bsd', _ctx_2048c, _ctx_2048P)
        _ctx_2048t = _ctx_2048t * jax.lax.rsqrt(jnp.mean(jnp.square(_ctx_2048t)) + 1e-12) * 0.953939
        ctx_2048 = -0.000292821 + 1.00034 * (_ctx_2048t + 0.3 * jax.random.normal(jax.random.fold_in(_rk, 611), (8, 128, 256), jnp.float32))
        _g = jax.random.normal(jax.random.fold_in(_rk, 9001), (2, 2), jnp.float32)
        _g = jnp.sign(_g) * jnp.maximum(jnp.abs(_g), 1.0) + (_g == 0) * 1.0
        g_xattn = _g[0]
        g_ffn = _g[1]
        return (x, ctx_2048, g_xattn, g_ffn)
    x, ctx_2048, g_xattn, g_ffn = _rec_inputs()

    def _L0_xattn_setup():
        import jax, jax.numpy as jnp
        import numpy as np
        key = jax.random.key(seed)
        k1, k2, k3, k4, k5 = jax.random.split(key, 5)
        B, D_MODEL, L = (2, 128, 256)
        HEAD_DIM = 8
        H = D_MODEL // HEAD_DIM
        return {'k': jax.random.normal(k1, (B, D_MODEL, L), dtype=jnp.float32), 'v': jax.random.normal(k2, (B, D_MODEL, L), dtype=jnp.float32), 'q': jax.random.normal(k3, (B, D_MODEL, L), dtype=jnp.float32), 'ssm_kernel': jax.random.normal(k4, (H, L), dtype=jnp.float32), 'D': jax.random.normal(k5, (H,), dtype=jnp.float32), 'head_dim': HEAD_DIM}
    _L0_xattn_all = _L0_xattn_setup()
    _L0_xattn_in = {k: v for k, v in _L0_xattn_all.items() if k in ('ssm_kernel', 'D')}
    del _L0_xattn_all

    def _L0_ffn_setup():
        import jax, jax.numpy as jnp
        import numpy as np
        H = 256
        E = 8
        TOPK = 2
        I_MOE = 128
        I_SH = 512

        def _silu_and_mul(gu):
            g, u = jnp.split(gu, 2, axis=-1)
            return jax.nn.silu(g) * u
        key = jax.random.key(seed)
        ks = jax.random.split(key, 6)
        s = lambda *sh: 1.0 / np.sqrt(sh[-2])
        hidden_states = jax.random.normal(ks[0], (2, 128, H), dtype=jnp.float32)
        w_gate = jax.random.normal(ks[1], (H, E), dtype=jnp.float32) * (1.0 / np.sqrt(H))
        w_gate_up = jax.random.normal(ks[2], (E, H, 2 * I_MOE), dtype=jnp.float32) * (1.0 / np.sqrt(H))
        w_down = jax.random.normal(ks[3], (E, I_MOE, H), dtype=jnp.float32) * (1.0 / np.sqrt(I_MOE))
        w_sh_gate_up = jax.random.normal(ks[4], (H, 2 * I_SH), dtype=jnp.float32) * (1.0 / np.sqrt(H))
        w_sh_down = jax.random.normal(ks[5], (I_SH, H), dtype=jnp.float32) * (1.0 / np.sqrt(I_SH))
        return {'hidden_states': hidden_states, 'w_gate': w_gate, 'w_gate_up': w_gate_up, 'w_down': w_down, 'w_sh_gate_up': w_sh_gate_up, 'w_sh_down': w_sh_down}
    _L0_ffn_all = _L0_ffn_setup()
    _L0_ffn_in = {k: v for k, v in _L0_ffn_all.items() if k in ('w_gate', 'w_gate_up', 'w_down', 'w_sh_gate_up', 'w_sh_down')}
    del _L0_ffn_all

    def _L1_xattn_setup():
        import math
        import jax, jax.numpy as jnp
        import numpy as np
        HEADS = 16
        MASKED_BIAS = -10000.0

        def _mha(q, k, v):
            B, Sq, D = q.shape
            Sk = k.shape[-2]
            hd = D // HEADS
            qh = q.reshape(B, Sq, HEADS, hd).transpose(0, 2, 1, 3)
            kh = k.reshape(B, Sk, HEADS, hd).transpose(0, 2, 1, 3)
            vh = v.reshape(B, Sk, HEADS, hd).transpose(0, 2, 1, 3)
            scores = jnp.einsum('bhqd,bhkd->bhqk', qh, kh) / math.sqrt(hd)
            qi = jnp.arange(Sq)[:, None] + (Sk - Sq)
            ki = jnp.arange(Sk)[None, :]
            causal = ki <= qi
            scores = jnp.where(causal[None, None], scores, jnp.asarray(MASKED_BIAS, scores.dtype))
            attn = jax.nn.softmax(scores, axis=-1)
            out = jnp.einsum('bhqk,bhkd->bhqd', attn, vh)
            return out.transpose(0, 2, 1, 3).reshape(B, Sq, D)
        key = jax.random.key(seed)
        kq, kk, kv = jax.random.split(key, 3)
        B, S, D = (4, 128, 256)
        q = jax.random.normal(kq, (B, S, D), dtype=jnp.float32)
        k = jax.random.normal(kk, (B, S, D), dtype=jnp.float32)
        v = jax.random.normal(kv, (B, S, D), dtype=jnp.float32)
        return {'q': q, 'k': k, 'v': v}
    _L1_xattn_all = _L1_xattn_setup()
    _L1_xattn_in = {k: v for k, v in _L1_xattn_all.items() if k in ()}
    del _L1_xattn_all

    def _L1_ffn_setup():
        import jax, jax.numpy as jnp
        import numpy as np
        H = 256
        M = 176
        E = 32
        TOPK = 6
        G = 8
        TOPK_G = 4
        SH = 2
        B, S = (1, 128)
        key = jax.random.key(seed)
        ks = jax.random.split(key, 9)
        sc = 0.02
        return {'x': jax.random.normal(ks[0], (B, S, H), dtype=jnp.float32), 'w_router': jax.random.normal(ks[1], (H, E), dtype=jnp.float32) * sc, 'corr_bias': jax.random.normal(ks[2], (E,), dtype=jnp.float32) * 0.1, 'gate_w': jax.random.normal(ks[3], (E, H, M), dtype=jnp.float32) * sc, 'up_w': jax.random.normal(ks[4], (E, H, M), dtype=jnp.float32) * sc, 'down_w': jax.random.normal(ks[5], (E, M, H), dtype=jnp.float32) * sc, 'sh_gate_w': jax.random.normal(ks[6], (H, M * SH), dtype=jnp.float32) * sc, 'sh_up_w': jax.random.normal(ks[7], (H, M * SH), dtype=jnp.float32) * sc, 'sh_down_w': jax.random.normal(ks[8], (M * SH, H), dtype=jnp.float32) * sc}
    _L1_ffn_all = _L1_ffn_setup()
    _L1_ffn_in = {k: v for k, v in _L1_ffn_all.items() if k in ('w_router', 'corr_bias', 'gate_w', 'up_w', 'down_w', 'sh_gate_w', 'sh_up_w', 'sh_down_w')}
    del _L1_ffn_all
    return {'x': x, 'ctx_2048': ctx_2048, 'g_xattn': g_xattn, 'g_ffn': g_ffn, 'L0_xattn_ssm_kernel': _L0_xattn_in['ssm_kernel'], 'L0_xattn_D': _L0_xattn_in['D'], 'L0_ffn_w_gate': _L0_ffn_in['w_gate'], 'L0_ffn_w_gate_up': _L0_ffn_in['w_gate_up'], 'L0_ffn_w_down': _L0_ffn_in['w_down'], 'L0_ffn_w_sh_gate_up': _L0_ffn_in['w_sh_gate_up'], 'L0_ffn_w_sh_down': _L0_ffn_in['w_sh_down'], 'L1_ffn_w_router': _L1_ffn_in['w_router'], 'L1_ffn_corr_bias': _L1_ffn_in['corr_bias'], 'L1_ffn_gate_w': _L1_ffn_in['gate_w'], 'L1_ffn_up_w': _L1_ffn_in['up_w'], 'L1_ffn_down_w': _L1_ffn_in['down_w'], 'L1_ffn_sh_gate_w': _L1_ffn_in['sh_gate_w'], 'L1_ffn_sh_up_w': _L1_ffn_in['sh_up_w'], 'L1_ffn_sh_down_w': _L1_ffn_in['sh_down_w']}

def reference(x, ctx_2048, g_xattn, g_ffn, L0_xattn_ssm_kernel, L0_xattn_D, L0_ffn_w_gate, L0_ffn_w_gate_up, L0_ffn_w_down, L0_ffn_w_sh_gate_up, L0_ffn_w_sh_down, L1_ffn_w_router, L1_ffn_corr_bias, L1_ffn_gate_w, L1_ffn_up_w, L1_ffn_down_w, L1_ffn_sh_gate_w, L1_ffn_sh_up_w, L1_ffn_sh_down_w):
    import jax
    import jax.numpy as jnp

    def _L0_xattn_ref(k, v, q, ssm_kernel, D, head_dim):
        import jax, jax.numpy as jnp
        import numpy as np
        B, HD, L = k.shape
        H = HD // head_dim
        fft_size = 2 * L
        k_ = k.reshape(B, H, head_dim, L)
        v_ = v.reshape(B, H, head_dim, L)
        q_ = q.reshape(B, H, head_dim, L)
        kv = jnp.einsum('bhil,bhjl->bijhl', k_, v_)
        kv_f = jnp.fft.rfft(kv, n=fft_size)
        kernel_f = jnp.fft.rfft(ssm_kernel, n=fft_size)
        y = jnp.fft.irfft(kv_f * kernel_f, n=fft_size)[..., :L]
        out = y + kv * D[None, None, None, :, None]
        out = jnp.einsum('bijhl,bhil->bjhl', out, q_)
        out = jnp.transpose(out, (0, 2, 1, 3)).reshape(B, H * head_dim, L)
        return out.astype(k.dtype)

    def _L0_ffn_ref(hidden_states, w_gate, w_gate_up, w_down, w_sh_gate_up, w_sh_down):
        import jax, jax.numpy as jnp
        import numpy as np
        H = 256
        E = 8
        TOPK = 2
        I_MOE = 128
        I_SH = 512

        def _silu_and_mul(gu):
            g, u = jnp.split(gu, 2, axis=-1)
            return jax.nn.silu(g) * u
        orig_shape = hidden_states.shape
        x = hidden_states.reshape(-1, orig_shape[-1])
        router_logits = x @ w_gate
        probs = jax.nn.softmax(router_logits, axis=-1)
        topk_w, topk_ids = jax.lax.top_k(probs, TOPK)
        topk_w = topk_w / jnp.sum(topk_w, axis=-1, keepdims=True)
        combine = jnp.sum(topk_w[..., None] * jax.nn.one_hot(topk_ids, E, dtype=x.dtype), axis=1)
        gu = jnp.einsum('th,ehf->etf', x, w_gate_up)
        act = _silu_and_mul(gu)
        eo = jnp.einsum('eti,eih->eth', act, w_down)
        routed = jnp.einsum('te,eth->th', combine, eo)
        shared = _silu_and_mul(x @ w_sh_gate_up) @ w_sh_down
        return (routed + shared).reshape(orig_shape)

    def _L1_xattn_ref(q, k, v):
        import math
        import jax, jax.numpy as jnp
        import numpy as np
        HEADS = 16
        MASKED_BIAS = -10000.0

        def _mha(q, k, v):
            B, Sq, D = q.shape
            Sk = k.shape[-2]
            hd = D // HEADS
            qh = q.reshape(B, Sq, HEADS, hd).transpose(0, 2, 1, 3)
            kh = k.reshape(B, Sk, HEADS, hd).transpose(0, 2, 1, 3)
            vh = v.reshape(B, Sk, HEADS, hd).transpose(0, 2, 1, 3)
            scores = jnp.einsum('bhqd,bhkd->bhqk', qh, kh) / math.sqrt(hd)
            qi = jnp.arange(Sq)[:, None] + (Sk - Sq)
            ki = jnp.arange(Sk)[None, :]
            causal = ki <= qi
            scores = jnp.where(causal[None, None], scores, jnp.asarray(MASKED_BIAS, scores.dtype))
            attn = jax.nn.softmax(scores, axis=-1)
            out = jnp.einsum('bhqk,bhkd->bhqd', attn, vh)
            return out.transpose(0, 2, 1, 3).reshape(B, Sq, D)
        return _mha(q, k, v)

    def _L1_ffn_ref(x, w_router, corr_bias, gate_w, up_w, down_w, sh_gate_w, sh_up_w, sh_down_w):
        import jax, jax.numpy as jnp
        import numpy as np
        H = 256
        M = 176
        E = 32
        TOPK = 6
        G = 8
        TOPK_G = 4
        SH = 2
        B, S = (1, 128)
        b, s, h = x.shape
        xf = x.reshape(-1, h)
        T = xf.shape[0]
        logits = xf @ w_router
        scores = jax.nn.sigmoid(logits)
        sfc = scores + corr_bias
        grp = sfc.reshape(T, G, E // G)
        top2, _ = jax.lax.top_k(grp, 2)
        group_scores = top2.sum(-1)
        _, gidx = jax.lax.top_k(group_scores, TOPK_G)
        group_mask = jax.nn.one_hot(gidx, G, dtype=jnp.float32).sum(axis=1) > 0
        score_mask = jnp.repeat(group_mask, E // G, axis=1)
        masked = jnp.where(score_mask, sfc, -jnp.inf)
        _, topk_idx = jax.lax.top_k(masked, TOPK)
        topk_w = jnp.take_along_axis(scores, topk_idx, axis=1)
        combine = jnp.zeros((T, E), dtype=x.dtype).at[jnp.arange(T)[:, None], topk_idx].add(topk_w)
        g = jnp.einsum('th,ehm->etm', xf, gate_w)
        u = jnp.einsum('th,ehm->etm', xf, up_w)
        eo = jnp.einsum('etm,emh->eth', jax.nn.silu(g) * u, down_w)
        routed = jnp.einsum('te,eth->th', combine, eo)
        shared = jax.nn.silu(xf @ sh_gate_w) * (xf @ sh_up_w) @ sh_down_w
        return (routed + shared).reshape(b, s, h)
    x = x + jnp.tanh(g_xattn[0]) * _L0_xattn_ref(ctx_2048, ctx_2048, _layernorm(x, axis=-1), L0_xattn_ssm_kernel, L0_xattn_D, 8)
    x = x + jnp.tanh(g_ffn[0]) * _L0_ffn_ref(_layernorm(x, axis=-1), L0_ffn_w_gate, L0_ffn_w_gate_up, L0_ffn_w_down, L0_ffn_w_sh_gate_up, L0_ffn_w_sh_down)
    x = x + jnp.tanh(g_xattn[1]) * _L1_xattn_ref(_layernorm(x, axis=-1), ctx_2048, ctx_2048)
    x = x + jnp.tanh(g_ffn[1]) * _L1_ffn_ref(_layernorm(x, axis=-1), L1_ffn_w_router, L1_ffn_corr_bias, L1_ffn_gate_w, L1_ffn_up_w, L1_ffn_down_w, L1_ffn_sh_gate_w, L1_ffn_sh_up_w, L1_ffn_sh_down_w)
    return x

_drawn_inputs = setup_inputs


def setup_inputs(seed=0):
    import zlib

    import numpy as np

    out = dict(_drawn_inputs(seed))
    spreads = {'g_ffn': (-1.0, 0.6)}
    factors = {'L0_ffn_w_gate': 5.393,
     'L0_ffn_w_gate_up': 4.798,
     'L0_ffn_w_down': 4.773,
     'L0_ffn_w_sh_gate_up': 3.56,
     'L0_ffn_w_sh_down': 3.561,
     'L1_ffn_w_router': 8.0,
     'L1_ffn_corr_bias': 8.0,
     'L1_ffn_gate_w': 8.0,
     'L1_ffn_up_w': 8.0,
     'L1_ffn_down_w': 8.0,
     'L1_ffn_sh_gate_w': 8.0,
     'L1_ffn_sh_up_w': 8.0,
     'L1_ffn_sh_down_w': 8.0}
    for name, (base, spread) in spreads.items():
        noise = np.random.default_rng([zlib.crc32(name.encode()), seed]).standard_normal(out[name].shape)
        drawn = base * np.exp(spread * noise) if base else spread * noise
        out[name] = jnp.asarray(drawn.astype(out[name].dtype))
    for name, factor in factors.items():
        out[name] = (out[name] * factor).astype(out[name].dtype)
    return out
```

```python
from contextlib import ExitStack

import numpy as np

import concourse.bass as bass
from concourse import mybir
from concourse.alu_op_type import AluOpType as ALU

F32 = mybir.dt.float32
F32R = mybir.dt.float32r
BF16 = mybir.dt.bfloat16
U32 = mybir.dt.uint32
ACT = mybir.ActivationFunctionType
AX = mybir.AxisListType

P = 128
B, S, D = 8, 128, 256
T = B * S
KT = D // P
HALF = 512
NHALF = T // HALF
HB = HALF // S
A_HEADS, A_HD = 16, 8
C_HEADS, C_HD = 16, 16
TH = P // C_HD
HQ = 4
NQ = C_HEADS // HQ
EPS = 1e-5
RSQRT_MAGIC = 0x5F3759DF
MASK = -10000.0 * C_HD ** 0.5
LOWEST = -3.0e38

EXPERTS = [8, 32]
TOPK = [2, 6]
GROUPS, GSIZE, TOPG = 8, 4, 4
HID = [128, 176]
SHARED = [4, 3]
ROUTED = [E * M // P for E, M in zip(EXPERTS, HID)]
NT = [s + r for s, r in zip(SHARED, ROUTED)]
CHUNK = 16
GU = 2 * KT * P
WCOLS = GU + D


def build(nc, a, out):
    with ExitStack() as ctx:
        def sb(name, shape, dt=F32):
            return ctx.enter_context(nc.sbuf_tensor(name, shape, dt))

        def sem(name):
            return ctx.enter_context(nc.semaphore(name))

        X = sb("X", [P, B, D])
        xh = sb("xh", [P, B, D])
        xT_hi = sb("xT_hi", [P, KT, T], F32R)
        xT_lo = sb("xT_lo", [P, KT, T], F32R)
        ident = sb("ident", [P, P])
        ident_bf = sb("ident_bf", [P, P], BF16)
        gates = sb("gates", [P, 4])
        tgates = sb("tgates", [P, 4])
        bnst = sb("bnst", [P, B, 6])
        mv = sb("mv", [P, B, 2])
        rstd = sb("rstd", [P, B])
        nt1 = sb("nt1", [P, B])
        nt2 = sb("nt2", [P, B])
        magic = sb("magic", [P, B], U32)
        V = sb("V", [P, B, C_HEADS, C_HD + 1])
        KBD = sb("KBD", [P, B, KT, TH, S])
        cmask = sb("cmask", [P, HQ, S], BF16)
        anti = sb("anti", [P, D])
        skipD = sb("skipD", [P, A_HEADS])
        w_raw = sb("w_raw", [P, 2, WCOLS])
        bias1 = sb("bias1", [P, EXPERTS[1]])
        wr = [sb(f"wr{n}", [P, KT, EXPERTS[n]]) for n in range(2)]
        wr_hi = [sb(f"wr_hi{n}", [P, KT, EXPERTS[n]], F32R) for n in range(2)]
        wr_lo = [sb(f"wr_lo{n}", [P, KT, EXPERTS[n]], F32R) for n in range(2)]
        h_hi = [sb(f"h_hi{k}", [P, T], F32R) for k in range(2)]
        h_lo = [sb(f"h_lo{k}", [P, T], F32R) for k in range(2)]
        w_hi = [sb(f"w_hi{k}", [P, WCOLS], F32R) for k in range(2)]
        w_lo = [sb(f"w_lo{k}", [P, WCOLS], F32R) for k in range(2)]

        ARENA = 15 * 1024
        arena = sb("arena", [P, ARENA])
        at = [0]

        def take(*shape):
            n = int(np.prod(shape))
            v = arena[:, at[0]:at[0] + n]
            at[0] += n
            assert at[0] <= ARENA, at[0]
            if len(shape) == 1:
                return v
            names = "abcd"[:len(shape)]
            return v.rearrange(f"p ({' '.join(names)}) -> p {' '.join(names)}", **dict(zip(names, shape)))

        kT = take(KT, B, S)
        toep = take(A_HEADS, D)
        toepD = [take(D) for _ in range(2)]
        kv = [take(KT * B, A_HD, A_HD) for _ in range(2)]
        prod = [take(KT * B, A_HD, A_HD) for _ in range(2)]
        qT = take(KT, T)
        oA = take(KT * B, S)
        at[0] = 0
        sg = take(T)
        hh = take(T)
        cb = [take(T) for _ in range(2)]
        combT = take(T)
        yT = take(KT, T)
        rt = [take(B, EXPERTS[1]) for _ in range(8)]
        scan = [take(B, 16 + EXPERTS[1]) for _ in range(2)]
        top8 = take(B, 8)
        rs = [take(B) for _ in range(3)]
        comb = take(B, EXPERTS[1])
        gmask = take(B, GROUPS)
        at[0] = 0
        Sm = [take(HQ, S) for _ in range(2)]
        Pm = [[take(HQ, S) for _ in range(NQ)] for _ in range(2)]
        PTs = [take(HQ, S) for _ in range(2)]
        qc = [take(KT, S) for _ in range(2)]
        xr = [take(D) for _ in range(2)]
        mx = [take(HQ) for _ in range(2)]
        oC = take(C_HEADS, C_HD)
        rC = [take(C_HEADS) for _ in range(2)]

        psum = ctx.enter_context(nc.psum_tensor("psum", [P, 8, HALF], F32))
        bank = [psum[:, k, :] for k in range(8)]

        in_x, in_kT, in_V, in_gates, in_small, in_kbd = (sem(n) for n in
            ("in_x", "in_kT", "in_V", "in_gates", "in_small", "in_kbd"))
        in_toep = [sem(f"in_toep{k}") for k in range(2)]
        pool_const, pool_kbd0, pool_v1 = sem("pool_const"), sem("pool_kbd0"), sem("pool_v1")
        dve_step = sem("dve_step")
        act_gates = sem("act_gates")
        norm_ready = sem("norm_ready")
        xt_ready = sem("xt_ready")
        xt_out = sem("xt_out")
        xlo_ready = sem("xlo_ready")
        wr_hi_done, wr_lo_done = sem("wr_hi_done"), sem("wr_lo_done")
        kv_ready, toepD_ready, conv_done, prod_ready, conv_out = (sem(n) for n in
            ("kv_ready", "toepD_ready", "conv_done", "prod_ready", "conv_out"))
        oT_ready = sem("oT_ready")
        x_new = sem("x_new")

        names = ("logits", "logits_kept", "router_in", "router_act", "comb_ready", "comb_T", "comb_copied",
                 "comb_out", "whi_gu", "whi_d", "wlo_gu", "wlo_d", "gu_done", "down_done", "silu_done",
                 "sc_done", "h_done", "hhi_done", "hlo_done", "y_copied", "yT_ready")
        L = [{name: sem(f"{name}{n}") for name in names} for n in range(2)]
        w_in = [[sem(f"w_in{n}_{k}") for k in range(2)] for n in range(2)]
        c_in = [[sem(f"c_in{n}_{k}") for k in range(2)] for n in range(2)]
        (xr_ready, q_T, q_out, s_ready, mx_ready, sm_ready, exp_done, pt_ready, pt_out, pv_ready, o_out) = (
            sem(n) for n in ("xr_ready", "q_T", "q_out", "s_ready", "mx_ready", "sm_ready", "exp_done",
                             "pt_ready", "pt_out", "pv_ready", "o_out"))
        out_done = sem("out_done")

        comb_dram = [nc.dram_tensor("comb_rows0", (EXPERTS[0], T), F32, kind="Internal").ap(),
                     nc.dram_tensor("comb_rows1", (ROUTED[1] * P // CHUNK, T), F32, kind="Internal").ap()]

        def over(ap, *shape):
            return ap.unsqueeze(len(ap.shape)).broadcast_to([*ap.shape, shape[0]])

        NORMS_AHEAD = [0, B, 2 * B]
        routed_pairs = [ROUTED[n] // 2 for n in range(2)]

        block = ctx.enter_context(nc.Block())

        @block.sync
        def _(sp):
            sp.dma_start(kT, a["ctx_T_rev"]).then_inc(in_kT, 16)
            toep_src = a["lags"]
            def toeplitz(h0, n):
                return bass.AP(toep_src.tensor, toep_src.offset + h0 * (P + D) + 1, [[1, P], [P + D, n], [1, D]])
            sp.dma_start(toep[:, 0:2, :], toeplitz(0, 2)).then_inc(in_toep[0], 16)
            sp.dma_start(X[:], a["x"].rearrange("b s d -> s b d")).then_inc(in_x, 16)
            sp.dma_start(toep[:, 2:, :], toeplitz(2, A_HEADS - 2)).then_inc(in_toep[1], 16)
            for k in range(2):
                sp.dma_start(w_raw[:, k, :], a["w0"][k]).then_inc(w_in[0][k], 16)
            sp.dma_start(V[:], a["ctx_v"]).then_inc(in_V, 16)
            sp.wait_ge(pool_kbd0, 1)
            for h in range(TH):
                rows = slice(h * C_HD, (h + 1) * C_HD)
                for t in range(KT):
                    sp.dma_start(KBD[rows, :, t, h, :], a["ctx_T"][t, rows]).then_inc(in_kbd, 16)

            def expert_loads(n):
                q, R = L[n], ROUTED[n]

                def weights(t, k):
                    sp.wait_ge(q["wlo_d"], t + 1)
                    sp.dma_start(w_raw[:, k, :], a[f"w{n}"][t + 2]).then_inc(w_in[n][k], 16)

                def combine(r, k):
                    if n == 0:
                        src = comb_dram[0][r].unsqueeze(0).broadcast_to([P, T])
                        sp.dma_start(cb[k], src).then_inc(c_in[n][k], 16)
                    else:
                        c = P // CHUNK
                        src = comb_dram[1][bass.ds(r * c, c), :].unsqueeze(1).broadcast_to([c, CHUNK, T])
                        sp.dma_start(cb[k], src).then_inc(c_in[n][k], 16)

                for t in range(2):
                    weights(t, t)
                sp.wait_ge(q["comb_copied"], 2)
                if n == 0:
                    sp.dma_start(comb_dram[0], combT[0:EXPERTS[0], :]).then_inc(q["comb_out"], 16)
                else:
                    rep = HID[1] // CHUNK
                    sp.dma_start(comb_dram[1].rearrange("(e c) t -> e c t", c=rep),
                                 combT[0:EXPERTS[1], :].unsqueeze(1).broadcast_to([EXPERTS[1], rep, T])
                                 ).then_inc(q["comb_out"], 16)
                sp.wait_ge(q["comb_out"], 16)
                for k in range(2):
                    combine(k, k)
                for t in range(2, SHARED[n]):
                    weights(t, t % 2)
                with sp.Fori(0, routed_pairs[n] - 1) as i:
                    for k in range(2):
                        t = 2 * i + (SHARED[n] + k)
                        weights(t, (SHARED[n] + k) % 2)
                        sp.wait_ge(q["sc_done"], 4 * i + 2 * (k + 1))
                        combine(2 * i + (k + 2), k)

            expert_loads(0)
            sp.wait_ge(L[0]["wlo_d"], NT[0])
            for k in range(2):
                sp.dma_start(w_raw[:, k, :], a["w1"][k]).then_inc(w_in[1][k], 16)
            expert_loads(1)
            for q in range(B // 2):
                sp.wait_ge(x_new, 8 + q + 1)
                sp.dma_start(out[2 * q:2 * q + 2].rearrange("b s d -> s b d"), X[:, 2 * q:2 * q + 2, :]).then_inc(out_done, 16)
            sp.wait_ge(out_done, 16 * (B // 2))

        @block.gpsimd
        def _(pool):
            pool.memset(ident[:], 0.0).then_inc(pool_const, 1)
            pool.memset(ident_bf[:], 0.0).then_inc(pool_const, 1)
            pool.memset(anti[:], 0.0).then_inc(pool_const, 1)
            pool.memset(cmask[:], 0.0).then_inc(pool_const, 1)
            pool.wait_ge(pool_const, 4)
            pool.affine_select(out=anti[:], in_=anti[:], compare_op=ALU.not_equal, fill=1.0,
                               base=-(P - 1), pattern=[[1, D]], channel_multiplier=1).then_inc(pool_const, 1)
            for m in (ident, ident_bf):
                pool.affine_select(out=m[:], in_=m[:], compare_op=ALU.not_equal, fill=1.0,
                                   base=0, pattern=[[-1, P]], channel_multiplier=1).then_inc(pool_const, 1)
            pool.affine_select(out=cmask[:], in_=cmask[:], compare_op=ALU.is_ge, fill=MASK,
                               base=0, pattern=[[0, HQ], [-1, S]], channel_multiplier=1).then_inc(pool_const, 1)
            pool.dma_start(gates[:], a["gates"].unsqueeze(0).broadcast_to([P, 4])).then_inc(in_gates, 16)
            pool.dma_start(skipD[:], a["skip"].unsqueeze(0).broadcast_to([P, A_HEADS])).then_inc(in_gates, 16)
            pool.dma_start(bias1[:], a["bias1"].unsqueeze(0).broadcast_to([P, EXPERTS[1]])).then_inc(in_small, 16)
            for n in range(2):
                pool.dma_start(wr[n][:], a[f"wr{n}"]).then_inc(in_small, 16)

            kT3 = kT.rearrange("p t b s -> p (t b) s")

            def key_value(h, k, first):
                if not first:
                    pool.wait_ge(conv_done, h - 1)
                src = kT3[:, :, bass.ds(h * A_HD, A_HD)]
                pool.tensor_tensor(kv[k], src.unsqueeze(3).broadcast_to([P, KT * B, A_HD, A_HD]),
                                   src.unsqueeze(2).broadcast_to([P, KT * B, A_HD, A_HD]), ALU.mult).then_inc(kv_ready, 1)

            pool.wait_ge(in_kT, 16)
            for k in range(2):
                key_value(k, k, True)
            with pool.Fori(1, A_HEADS // 2) as i:
                for k in range(2):
                    key_value(2 * i + k, k, False)
            pool.memset(KBD[:], 0.0).then_inc(pool_kbd0, 1)
            pool.wait_ge(in_V, 16)
            pool.memset(V[:, :, :, C_HD:], 1.0).then_inc(pool_v1, 1)

        @block.scalar
        def _(act):
            act.wait_ge(in_gates, 32)
            act.activation(tgates[:], gates[:], ACT.Tanh).then_inc(act_gates, 1)

            for n, (h, t) in enumerate((h, t) for h in range(2) for t in range(KT)):
                act.wait_ge(xt_ready, n + 1)
                act.copy(qT[:, t, h * HALF:(h + 1) * HALF], bank[2 * t + h]).then_inc(xt_out, 1)
            act.wait_ge(in_small, 48)
            for n in range(2):
                act.copy(wr_hi[n][:], wr[n][:]).then_inc(wr_hi_done, 1)

            def experts(n, transposed):
                q, S0, N = L[n], SHARED[n], NT[n]

                def split_gu(t, k, landed=None):
                    act.wait_ge(w_in[n][k], 16 * (t // 2 + 1) if landed is None else landed)
                    if not (isinstance(t, int) and t < 2):
                        act.wait_ge(q["gu_done"], 2 * t - 2)
                    act.copy(w_hi[k][:, :GU], w_raw[:, k, :GU]).then_inc(q["whi_gu"], 1)

                def step(t, k, landed=None, last=False):
                    if not last:
                        split_gu(t + 1, 1 - k, landed)
                    if not (isinstance(t, int) and t < 2):
                        act.wait_ge(q["down_done"], t - 1)
                    act.copy(w_hi[k][:, GU:], w_raw[:, k, GU:]).then_inc(q["whi_d"], 1)
                    for h in range(NHALF):
                        act.wait_ge(q["gu_done"], 2 * t + (h + 1))
                        act.activation(sg[:, h * HALF:(h + 1) * HALF], bank[2 * h], ACT.Silu).then_inc(q["silu_done"], 1)
                    for h in range(NHALF):
                        cols = slice(h * HALF, (h + 1) * HALF)
                        act.wait_ge(q["h_done"], 2 * t + (h + 1))
                        act.copy(h_hi[k][:, cols], hh[:, cols]).then_inc(q["hhi_done"], 1)

                for m, (h, t) in enumerate((h, t) for h in range(2) for t in range(KT)):
                    act.wait_ge(xt_ready, 4 * transposed + m + 1)
                    act.copy(xT_hi[:, t, h * HALF:(h + 1) * HALF], bank[2 * t + h]).then_inc(xt_out, 1)
                split_gu(0, 0)
                E = EXPERTS[n]
                if n == 0:
                    act.wait_ge(q["router_in"], 1)
                    act.activation(rt[1][:, :, 0:E], rt[0][:, :, 0:E], ACT.Exp).then_inc(q["router_act"], 1)
                else:
                    act.wait_ge(q["logits"], 1)
                    act.activation(rt[1][:, :, 0:E], bank[4][:, 0:B * E].rearrange("p (b e) -> p b e", b=B),
                                   ACT.Sigmoid).then_inc(q["logits_kept"], 1)
                for t in range(2):
                    step(t, t % 2)
                for h in range(NHALF):
                    act.wait_ge(q["comb_T"], h + 1)
                    act.copy(combT[0:E, h * HALF:(h + 1) * HALF], bank[h][0:E, :]).then_inc(q["comb_copied"], 1)
                for t in range(2, S0):
                    step(t, t % 2)
                with act.Fori(0, routed_pairs[n] - 1) as i:
                    for k in range(2):
                        step(2 * i + (S0 + k), (S0 + k) % 2, 16 * i + 16 * ((S0 + k + 1) // 2 + 1))
                step(N - 2, N % 2)
                step(N - 1, (N - 1) % 2, last=True)
                for t in range(KT):
                    for h in range(NHALF):
                        act.wait_ge(q["down_done"], N)
                        act.copy(yT[:, t, h * HALF:(h + 1) * HALF], bank[4 + 2 * t + h]).then_inc(q["y_copied"], 1)

            experts(0, 1)

            def queries(b, k):
                act.wait_ge(q_T, b + 1)
                act.copy(qc[k], bank[6][:, 0:D].rearrange("p (t s) -> p t s", t=KT)).then_inc(q_out, 1)

            def exponentials(b, k, j):
                act.wait_ge(sm_ready, NQ * b + (j + 1))
                act.activation(Pm[k][j], Sm[j % 2], ACT.Exp, scale=C_HD ** -0.5).then_inc(exp_done, 1)

            def attend(b, k, last=False, ahead=True):
                for j in range(NQ):
                    act.wait_ge(pt_ready, NQ * b + (j + 1))
                    act.copy(PTs[j % 2], bank[4 + j % 2].rearrange("p (h s) -> p h s", h=HQ)).then_inc(pt_out, 1)
                    if not last:
                        exponentials(b + 1, 1 - k, j)
                    if j == 1 and ahead:
                        queries(b + 2, k)

            for b in range(2):
                queries(b, b)
            for j in range(NQ):
                exponentials(0, 0, j)
            attend(0, 0)
            with act.Fori(0, 2) as i:
                for k in range(2):
                    attend(2 * i + (1 + k), (1 + k) % 2)
            attend(5, 1)
            attend(6, 0, ahead=False)
            attend(7, 1, last=True, ahead=False)

            experts(1, 2)

        @block.vector
        def _(dve):
            class Chain:
                def __init__(self):
                    self.n = 0

                def add(self, ins):
                    ins.then_inc(dve_step, 1)
                    self.n += 1

                def wait(self):
                    dve.wait_ge(dve_step, self.n)

                def link(self, ins):
                    self.add(ins)
                    self.wait()

            chain = Chain()
            link = chain.link
            link(dve.memset(magic[:], RSQRT_MAGIC + 1))

            def statistics():
                for b in range(B):
                    chain.add(dve.bn_stats(bnst[:, b, :], X[:, b, :]))
                chain.wait()
                for b in range(B):
                    chain.add(dve.bn_aggr(mv[:, b, :], bnst[:, b, :]))
                chain.wait()
                link(dve.tensor_scalar(nt2[:], mv[:, :, 1], EPS, None, ALU.add))
                link(dve.tensor_scalar(nt1[:].bitcast(U32), nt2[:].bitcast(U32), 1, 0xFFFFFFFF,
                                       ALU.logical_shift_right, ALU.bitwise_xor))
                link(dve.tensor_tensor(rstd[:].bitcast(U32), nt1[:].bitcast(U32), magic[:], ALU.add))
                for _ in range(4):
                    link(dve.scalar_tensor_tensor(out=nt1[:], in0=rstd[:], scalar=-0.5, in1=rstd[:], op0=ALU.mult, op1=ALU.mult))
                    link(dve.tensor_tensor(nt1[:], nt1[:], nt2[:], ALU.mult))
                    link(dve.scalar_tensor_tensor(out=rstd[:], in0=nt1[:], scalar=1.5, in1=rstd[:], op0=ALU.add, op1=ALU.mult))

            def layer_norm():
                statistics()
                for b in range(B):
                    dve.tensor_scalar(xh[:, b, :], X[:, b, :], mv[:, b, 0:1], rstd[:, b:b + 1],
                                      ALU.subtract, ALU.mult).then_inc(norm_ready, 1)

            def lag_zero(h, k, first):
                if not first:
                    dve.wait_ge(conv_done, h - 1)
                dve.scalar_tensor_tensor(out=toepD[k], in0=anti[:], scalar=skipD[:, bass.ds(h, 1)], in1=toep[:, bass.ds(h, 1), :].rearrange("p o d -> p (o d)"),
                                         op0=ALU.mult, op1=ALU.add).then_inc(toepD_ready, 1)

            q3 = qT.rearrange("p t (b s) -> p (t b) s", b=B)

            def contract(h, k):
                dve.wait_ge(conv_done, h + 1)
                y = psum[:, 4 + 2 * k:6 + 2 * k, :].rearrange("p t (b j i) -> p (t b) j i", b=B, j=A_HD)
                q = q3[:, :, bass.ds(h * A_HD, A_HD)].unsqueeze(2).broadcast_to([P, KT * B, A_HD, A_HD])
                dve.tensor_tensor(prod[k], y, q, ALU.mult).then_inc(prod_ready, 1)
                dve.wait_ge(prod_ready, h + 1)
                dve.tensor_reduce(oA[:, :, bass.ds(h * A_HD, A_HD)], prod[k], AX.X, ALU.add).then_inc(conv_out, 1)

            dve.wait_ge(in_toep[0], 16)
            dve.wait_ge(in_gates, 32)
            dve.wait_ge(pool_const, 8)
            for k in range(2):
                lag_zero(k, k, True)
            dve.wait_ge(in_x, 16)
            layer_norm()
            dve.wait_ge(in_toep[1], 16)
            dve.wait_ge(xt_out, 4)
            with dve.Fori(0, A_HEADS // 2 - 1) as i:
                for k in range(2):
                    contract(2 * i + k, k)
                    lag_zero(2 * i + (k + 2), k, False)
            for k in range(2):
                contract(A_HEADS - 2 + k, k)
            dve.wait_ge(act_gates, 1)

            def add_banks(ready, gate):
                for q in range(B // 2):
                    dve.wait_ge(ready, q + 1)
                    dve.scalar_tensor_tensor(out=X[:, 2 * q:2 * q + 2, :].rearrange("p b d -> p (b d)"), in0=bank[q],
                                             scalar=tgates[:, gate:gate + 1],
                                             in1=X[:, 2 * q:2 * q + 2, :].rearrange("p b d -> p (b d)"),
                                             op0=ALU.mult, op1=ALU.add).then_inc(x_new, 1)

            add_banks(oT_ready, 0)
            dve.wait_ge(x_new, 4)
            dve.wait_ge(wr_hi_done, 2)
            for n in range(2):
                dve.tensor_tensor(wr_lo[n][:], wr[n][:], wr_hi[n][:].bitcast(F32), ALU.subtract).then_inc(wr_lo_done, 1)

            def top_mask(v, E, K, sel):
                for b in range(B):
                    chain.add(dve.max(out=top8[:, b, :], in_=v[:, b, :]))
                chain.wait()
                kth = top8[:, :, K - 1:K].broadcast_to([P, B, E])
                eq = rt[7][:, :, 0:E]
                chain.add(dve.tensor_tensor(sel, v, kth, ALU.is_gt))
                chain.add(dve.tensor_tensor(eq, v, kth, ALU.is_equal))
                chain.wait()
                chain.add(dve.tensor_reduce(rs[0], sel, AX.X, ALU.add))
                chain.add(dve.tensor_copy(scan[0][:, :, 16:16 + E], eq))
                chain.wait()
                link(dve.tensor_scalar(rs[1], rs[0], -1.0, float(K), ALU.mult, ALU.add))
                cur, shift = 0, 1
                while shift < E:
                    link(dve.tensor_tensor(scan[1 - cur][:, :, 16:16 + E], scan[cur][:, :, 16:16 + E],
                                           scan[cur][:, :, 16 - shift:16 - shift + E], ALU.add))
                    cur, shift = 1 - cur, 2 * shift
                link(dve.tensor_tensor(scan[1 - cur][:, :, 16:16 + E], scan[cur][:, :, 16:16 + E], over(rs[1], E), ALU.is_le))
                link(dve.tensor_tensor(eq, eq, scan[1 - cur][:, :, 16:16 + E], ALU.mult))
                link(dve.tensor_tensor(sel, sel, eq, ALU.add))

            def softmax_in(q, E):
                logits = bank[4][:, 0:B * E].rearrange("p (b e) -> p b e", b=B)
                dve.wait_ge(q["logits"], 1)
                link(dve.tensor_reduce(rs[0], logits, AX.X, ALU.max))
                dve.tensor_tensor(rt[0][:, :, 0:E], logits, over(rs[0], E), ALU.subtract).then_inc(q["router_in"], 1)

            def route0(q):
                E, K = EXPERTS[0], TOPK[0]
                e, p, sel, c = (rt[k][:, :, 0:E] for k in (1, 2, 3, 4))
                dve.wait_ge(q["router_act"], 1)
                link(dve.tensor_reduce(rs[0], e, AX.X, ALU.add))
                link(dve.reciprocal(rs[1], rs[0]))
                link(dve.tensor_tensor(p, e, over(rs[1], E), ALU.mult))
                top_mask(p, E, K, sel)
                link(dve.tensor_tensor(c, p, sel, ALU.mult))
                link(dve.tensor_reduce(rs[0], c, AX.X, ALU.add))
                link(dve.reciprocal(rs[1], rs[0]))
                dve.tensor_tensor(comb[:, :, 0:E], c, over(rs[1], E), ALU.mult).then_inc(q["comb_ready"], 1)

            def route1(q):
                E, K = EXPERTS[1], TOPK[1]
                score, sfc, sel = rt[1], rt[2], rt[3]
                dve.wait_ge(q["logits_kept"], 1)
                link(dve.tensor_tensor(sfc, score, bias1[:].unsqueeze(1).broadcast_to([P, B, E]), ALU.add))
                pair = sfc.rearrange("p b (x y) -> p (b x) y", y=2)
                hi2, lo2 = (rt[k].rearrange("p b e -> p (b e)")[:, 0:B * GROUPS * 2] for k in (4, 5))
                chain.add(dve.tensor_tensor(hi2, pair[:, :, 0], pair[:, :, 1], ALU.max))
                chain.add(dve.tensor_tensor(lo2, pair[:, :, 0], pair[:, :, 1], ALU.min))
                chain.wait()
                hi2, lo2 = (v.rearrange("p (g y) -> p g y", y=2) for v in (hi2, lo2))
                t1, t2, t3 = (rt[k].rearrange("p b e -> p (b e)")[:, B * GROUPS * 2:B * GROUPS * 3] for k in (4, 5, 6))
                gs = rt[6].rearrange("p b e -> p (b e)")[:, 0:B * GROUPS]
                chain.add(dve.tensor_tensor(t1, hi2[:, :, 0], hi2[:, :, 1], ALU.max))
                chain.add(dve.tensor_tensor(t2, hi2[:, :, 0], hi2[:, :, 1], ALU.min))
                chain.add(dve.tensor_tensor(t3, lo2[:, :, 0], lo2[:, :, 1], ALU.max))
                chain.wait()
                link(dve.tensor_tensor(t2, t2, t3, ALU.max))
                link(dve.tensor_tensor(gs, t1, t2, ALU.add))
                top_mask(gs.rearrange("p (b g) -> p b g", b=B), GROUPS, TOPG, gmask)
                fill = rt[4].rearrange("p b e -> p (b e)")[:, 0:B * GROUPS]
                gm = gmask.rearrange("p b g -> p (b g)")
                link(dve.tensor_scalar(fill, gm, 1.0, -LOWEST, ALU.subtract, ALU.mult))
                s4 = sfc.rearrange("p b (g e) -> p (b g) e", e=GSIZE)
                link(dve.tensor_tensor(s4, s4, over(gm, GSIZE), ALU.mult))
                link(dve.tensor_tensor(s4, s4, over(fill, GSIZE), ALU.add))
                top_mask(sfc, E, K, sel)
                dve.tensor_tensor(comb, score, sel, ALU.mult).then_inc(q["comb_ready"], 1)

            def experts(n, transposed):
                q, S0, N = L[n], SHARED[n], NT[n]

                def split_gu(t, k):
                    dve.wait_ge(q["whi_gu"], t + 1)
                    dve.tensor_tensor(w_lo[k][:, :GU], w_raw[:, k, :GU], w_hi[k][:, :GU].bitcast(F32),
                                      ALU.subtract).then_inc(q["wlo_gu"], 1)

                def step(t, k, r=None, last=False):
                    if not last:
                        split_gu(t + 1, 1 - k)
                    dve.wait_ge(q["whi_d"], t + 1)
                    dve.tensor_tensor(w_lo[k][:, GU:], w_raw[:, k, GU:], w_hi[k][:, GU:].bitcast(F32),
                                      ALU.subtract).then_inc(q["wlo_d"], 1)
                    for h in range(NHALF):
                        cols = slice(h * HALF, (h + 1) * HALF)
                        dve.wait_ge(q["silu_done"], 2 * t + (h + 1))
                        if not isinstance(t, int) or t > 0:
                            dve.wait_ge(q["hlo_done"], 2 * t + (h - 1))
                        if r is None:
                            dve.tensor_tensor(hh[:, cols], sg[:, cols], bank[2 * h + 1], ALU.mult).then_inc(q["h_done"], 1)
                        else:
                            index, slot, landed = r
                            if h == 0:
                                dve.wait_ge(c_in[n][slot], landed)
                            dve.tensor_tensor(hh[:, cols], sg[:, cols], cb[slot][:, cols], ALU.mult).then_inc(q["sc_done"], 1)
                            dve.wait_ge(q["sc_done"], 2 * index + (h + 1))
                            dve.tensor_tensor(hh[:, cols], hh[:, cols], bank[2 * h + 1], ALU.mult).then_inc(q["h_done"], 1)
                    for h in range(NHALF):
                        cols = slice(h * HALF, (h + 1) * HALF)
                        dve.wait_ge(q["hhi_done"], 2 * t + (h + 1))
                        dve.tensor_tensor(h_lo[k][:, cols], hh[:, cols], h_hi[k][:, cols].bitcast(F32),
                                          ALU.subtract).then_inc(q["hlo_done"], 1)

                for m, (h, t) in enumerate((h, t) for h in range(2) for t in range(KT)):
                    cols = slice(h * HALF, (h + 1) * HALF)
                    dve.wait_ge(xt_out, 4 * transposed + m + 1)
                    dve.tensor_tensor(xT_lo[:, t, cols], bank[2 * t + h], xT_hi[:, t, cols].bitcast(F32),
                                      ALU.subtract).then_inc(xlo_ready, 1)
                split_gu(0, 0)
                for s in scan:
                    chain.add(dve.memset(s[:, :, 0:16], 0.0))
                if n == 0:
                    softmax_in(q, EXPERTS[0])
                step(0, 0)
                (route0 if n == 0 else route1)(q)
                for t in range(1, S0):
                    step(t, t % 2)
                with dve.Fori(0, routed_pairs[n] - 1) as i:
                    for k in range(2):
                        step(2 * i + (S0 + k), (S0 + k) % 2, (2 * i + k, k, 16 * i + 16))
                for k in range(2):
                    step(N - 2 + k, (N + k) % 2, (ROUTED[n] - 2 + k, k, 16 * routed_pairs[n]), last=k == 1)

            layer_norm()
            experts(0, 1)
            add_banks(L[0]["yT_ready"], 2)
            dve.wait_ge(x_new, 8)

            def normed(b, k):
                dve.tensor_scalar(xr[k], X[:, bass.ds(b, 1), :].rearrange("p o d -> p (o d)"), mv[:, bass.ds(b, 1), 0:1].rearrange("p o c -> p (o c)"), rstd[:, bass.ds(b, 1)],
                                  ALU.subtract, ALU.mult).then_inc(xr_ready, 1)

            def less_maximum(b, j, first=False):
                scores = bank[j].rearrange("p (h s) -> p h s", h=HQ)
                dve.wait_ge(s_ready, NQ * b + (j + 1))
                dve.tensor_reduce(mx[j % 2], scores, AX.X, ALU.max).then_inc(mx_ready, 1)
                dve.wait_ge(mx_ready, NQ * b + (j + 1))
                if not (first and j < 2):
                    dve.wait_ge(exp_done, NQ * b + (j - 1))
                dve.tensor_tensor(Sm[j % 2], scores, over(mx[j % 2], S), ALU.subtract).then_inc(sm_ready, 1)

            def add_heads(b):
                o = bank[7][:, 0:C_HEADS * (C_HD + 1)].rearrange("p (h c) -> p h c", h=C_HEADS)
                dve.wait_ge(pv_ready, b + 1)
                dve.reciprocal(rC[0], o[:, :, C_HD]).then_inc(o_out, 1)
                dve.wait_ge(o_out, 4 * b + 1)
                dve.tensor_scalar(rC[1], rC[0], tgates[:, 1:2], None, ALU.mult).then_inc(o_out, 1)
                dve.wait_ge(o_out, 4 * b + 2)
                dve.tensor_tensor(oC, o[:, :, 0:C_HD], over(rC[1], C_HD), ALU.mult).then_inc(o_out, 1)
                dve.wait_ge(o_out, 4 * b + 3)
                xb = X[:, bass.ds(b, 1), :].rearrange("p o d -> p (o d)")
                dve.tensor_tensor(xb, xb, oC.rearrange("p h c -> p (h c)"), ALU.add).then_inc(o_out, 1)

            statistics()
            for b in range(2):
                normed(b, b)
            for j in range(NQ):
                less_maximum(0, j, first=True)

            def attend(b, k, first=False, last=False, ahead=True):
                if not first:
                    add_heads(b - 1)
                if ahead:
                    dve.wait_ge(q_out, b + 1)
                    normed(b + 2, k)
                if not last:
                    for j in range(NQ):
                        less_maximum(b + 1, j)

            attend(0, 0, first=True)
            with dve.Fori(0, 2) as i:
                for k in range(2):
                    attend(2 * i + (1 + k), (1 + k) % 2)
            attend(5, 1)
            attend(6, 0, ahead=False)
            attend(7, 1, last=True, ahead=False)
            add_heads(7)
            dve.wait_ge(o_out, 4 * B)
            layer_norm()
            experts(1, 2)
            add_banks(L[1]["yT_ready"], 3)

        @block.tensor
        def _(pe):
            def transpose_norm(n):
                for h in range(NHALF):
                    for t in range(KT):
                        for b in range(h * HB, (h + 1) * HB):
                            pe.wait_ge(norm_ready, B * n + b + 1)
                            c = (b - h * HB) * S
                            mm = pe.transpose(bank[2 * t + h][:, c:c + S], xh[:, b, t * P:(t + 1) * P], ident[:])
                        mm.then_inc(xt_ready, 1)

            def convolve(h, k, first):
                pe.wait_ge(kv_ready, h + 1)
                pe.wait_ge(toepD_ready, h + 1)
                if not first:
                    pe.wait_ge(prod_ready, h - 1)
                near, far = toepD[k][:, 0:P], toepD[k][:, P:D]
                kv0, kv1 = (kv[k][:, t * B:(t + 1) * B].rearrange("p b j i -> p (b j i)") for t in range(KT))
                pe.matmul(bank[4 + 2 * k], near, kv0, start=True, stop=True)
                pe.matmul(bank[5 + 2 * k], far, kv0, start=True, stop=False)
                pe.matmul(bank[5 + 2 * k], near, kv1, start=False, stop=True).then_inc(conv_done, 1)

            for k in range(2):
                convolve(k, k, True)
            pe.wait_ge(pool_const, 8)
            transpose_norm(0)
            with pe.Fori(1, A_HEADS // 2) as i:
                for k in range(2):
                    convolve(2 * i + k, k, False)
            pe.wait_ge(conv_out, A_HEADS)
            for q in range(B // 2):
                for b in (2 * q, 2 * q + 1):
                    for t in range(KT):
                        c = (b % 2) * D + t * P
                        mm = pe.transpose(bank[q][:, c:c + P], oA[:, t * B + b, :], ident[:])
                mm.then_inc(oT_ready, 1)

            def experts(n, norm, transposed):
                q, S0, N, E = L[n], SHARED[n], NT[n], EXPERTS[n]
                transpose_norm(norm)

                def gate_up(t, k, first=False, half0_after=None):
                    pe.wait_ge(q["wlo_gu"], t + 1)
                    for h in range(NHALF):
                        if not first:
                            pe.wait_ge(q["silu_done"], 2 * t + (h - 1))
                            pe.wait_ge(q["h_done"], 2 * t + (h - 1))
                        x = slice(h * HALF, (h + 1) * HALF)
                        for g in range(2):
                            m = 0
                            for c in range(KT):
                                w = slice((g * KT + c) * P, (g * KT + c + 1) * P)
                                for wp, xp in ((w_hi[k], xT_hi), (w_hi[k], xT_lo), (w_lo[k], xT_hi)):
                                    mm = pe.matmul(bank[2 * h + g], wp[:, w], xp[:, c, x], start=m == 0, stop=m == 3 * KT - 1)
                                    m += 1
                        mm.then_inc(q["gu_done"], 1)

                def down(t, k, first=False, last=False):
                    pe.wait_ge(q["wlo_d"], t + 1)
                    for h in range(NHALF):
                        pe.wait_ge(q["hlo_done"], 2 * t + (h + 1))
                        x = slice(h * HALF, (h + 1) * HALF)
                        for c in range(KT):
                            w = slice(GU + c * P, GU + (c + 1) * P)
                            for m, (wp, hp) in enumerate(((w_hi[k], h_hi[k]), (w_hi[k], h_lo[k]), (w_lo[k], h_hi[k]))):
                                mm = pe.matmul(bank[4 + 2 * c + h], wp[:, w], hp[:, x], start=first and m == 0,
                                               stop=last and m == 2, skip_group_check=True)
                    mm.then_inc(q["down_done"], 1)

                pe.wait_ge(xlo_ready, 4 * (transposed - 1) + 4)
                pe.wait_ge(wr_lo_done, 2)
                for b in range(B):
                    m = 0
                    for c in range(KT):
                        for xp, wp in ((xT_hi, wr_hi[n]), (xT_hi, wr_lo[n]), (xT_lo, wr_hi[n])):
                            mm = pe.matmul(bank[4][:, b * E:(b + 1) * E], xp[:, c, b * S:(b + 1) * S], wp[:, c, :],
                                           start=m == 0, stop=m == 3 * KT - 1)
                            m += 1
                mm.then_inc(q["logits"], 1)
                gate_up(0, 0, first=True)
                gate_up(1, 1)
                pe.wait_ge(q["router_in" if n == 0 else "logits_kept"], 1)
                down(0, 0, first=True)
                pe.wait_ge(q["comb_ready"], 1)
                pe.wait_ge(q["silu_done"], 3)
                pe.wait_ge(q["h_done"], 3)
                for h in range(NHALF):
                    for b in range(h * HB, (h + 1) * HB):
                        c = (b - h * HB) * S
                        mm = pe.transpose(bank[h][0:E, c:c + S], comb[:, b, 0:E], ident[:])
                    mm.then_inc(q["comb_T"], 1)
                pe.wait_ge(q["comb_copied"], 2)
                for t in range(2, S0):
                    gate_up(t, t % 2)
                    down(t - 1, (t - 1) % 2)
                with pe.Fori(0, routed_pairs[n] - 1) as i:
                    for k in range(2):
                        gate_up(2 * i + (S0 + k), (S0 + k) % 2)
                        down(2 * i + (S0 + k - 1), (S0 + k - 1) % 2)
                for t in range(N - 2, N):
                    gate_up(t, t % 2)
                    down(t - 1, (t - 1) % 2)
                down(N - 1, (N - 1) % 2, last=True)
                for p in range(B // 2):
                    if p == 0:
                        pe.wait_ge(q["y_copied"], KT * NHALF)
                    for b in (2 * p, 2 * p + 1):
                        for t in range(KT):
                            c = (b % 2) * D + t * P
                            mm = pe.transpose(bank[p][:, c:c + P], yT[:, t, b * S:(b + 1) * S], ident[:])
                    mm.then_inc(q["yT_ready"], 1)

            experts(0, 1, 1)

            def queries(b, k):
                pe.wait_ge(xr_ready, b + 1)
                if not isinstance(b, int) or b > 0:
                    pe.wait_ge(q_out, b)
                for t in range(KT):
                    mm = pe.transpose(bank[6][:, t * S:(t + 1) * S], xr[k][:, t * P:(t + 1) * P], ident[:])
                mm.then_inc(q_T, 1)

            def scores(b, k, j, first=False):
                if j == 0:
                    pe.wait_ge(q_out, b + 1)
                if not first:
                    pe.wait_ge(sm_ready, NQ * b + (j + 1 - NQ))
                t, h = j // (NQ // KT), HQ * (j % (NQ // KT))
                pe.matmul(bank[j], ident_bf[:], cmask[:].rearrange("p h s -> p (h s)"), start=True, stop=False)
                pe.matmul(bank[j], qc[k][:, t, :], KBD[:, bass.ds(b, 1), t, h:h + HQ, :].rearrange("p o h s -> p (o h s)"),
                          start=False, stop=True).then_inc(s_ready, 1)

            def attend(b, k, first=False, last=False, ahead=True):
                for j in range(NQ):
                    if not last:
                        scores(b + 1, 1 - k, j)
                    pe.wait_ge(exp_done, NQ * b + (j + 1))
                    if not (first and j < 2):
                        pe.wait_ge(pt_out, NQ * b + (j - 1))
                    for h in range(HQ):
                        mm = pe.transpose(bank[4 + j % 2][:, h * S:(h + 1) * S], Pm[k][j][:, h, :], ident[:])
                    mm.then_inc(pt_ready, 1)
                    if j == 1 and ahead:
                        queries(b + 2, k)
                    pe.wait_ge(pt_out, NQ * b + (j + 1))
                    if j == 0 and not first:
                        pe.wait_ge(o_out, 4 * b - 1)
                    for h in range(HQ):
                        head = HQ * j + h
                        c = head * (C_HD + 1)
                        mm = pe.matmul(bank[7][:, c:c + C_HD + 1], PTs[j % 2][:, h, :],
                                       V[:, bass.ds(b, 1), head, :].rearrange("p o c -> p (o c)"), start=True, stop=True)
                mm.then_inc(pv_ready, 1)

            pe.wait_ge(pool_v1, 1)
            pe.wait_ge(in_kbd, 16 * TH * KT)
            for b in range(2):
                queries(b, b)
            for j in range(NQ):
                scores(0, 0, j, first=True)
            attend(0, 0, first=True)
            with pe.Fori(0, 2) as i:
                for k in range(2):
                    attend(2 * i + (1 + k), (1 + k) % 2)
            attend(5, 1)
            attend(6, 0, ahead=False)
            attend(7, 1, last=True, ahead=False)

            experts(1, 2, 2)


def _pack(gate, up, down):
    n = gate.shape[1] // P
    g, u = (w.reshape(KT, P, n, P).transpose(2, 1, 0, 3).reshape(n, P, KT * P) for w in (gate, up))
    return np.concatenate([g, u, down.reshape(n, P, D)], axis=2)


def _flat(w):
    return w.transpose(1, 0, 2).reshape(D, -1)


def _lay_out(i):
    pad = SHARED[1] * P - i["L1_ffn_sh_gate_w"].shape[1]
    ctx_T = np.ascontiguousarray(i["ctx_2048"].transpose(2, 0, 1)).reshape(KT, P, B, S)
    gu0, sgu0 = i["L0_ffn_w_gate_up"], i["L0_ffn_w_sh_gate_up"]
    m0, sh0 = HID[0], SHARED[0] * P
    ctx_v = np.ones((S, B, C_HEADS, C_HD + 1), np.float32)
    ctx_v[..., :C_HD] = i["ctx_2048"].transpose(1, 0, 2).reshape(S, B, C_HEADS, C_HD)
    return {
        "x": i["x"],
        "ctx_T": ctx_T,
        "ctx_T_rev": ctx_T[:, ::-1].transpose(1, 0, 2, 3),
        "ctx_v": ctx_v,
        "lags": np.pad(i["L0_xattn_ssm_kernel"], ((0, 0), (P, 0))),
        "skip": i["L0_xattn_D"],
        "gates": np.concatenate([i["g_xattn"], i["g_ffn"]]),
        "wr0": i["L0_ffn_w_gate"].reshape(KT, P, -1).transpose(1, 0, 2),
        "wr1": i["L1_ffn_w_router"].reshape(KT, P, -1).transpose(1, 0, 2),
        "bias1": i["L1_ffn_corr_bias"],
        "w0": _pack(np.concatenate([sgu0[:, :sh0], _flat(gu0[:, :, :m0])], axis=1),
                    np.concatenate([sgu0[:, sh0:], _flat(gu0[:, :, m0:])], axis=1),
                    np.concatenate([i["L0_ffn_w_sh_down"], i["L0_ffn_w_down"].reshape(-1, D)])),
        "w1": _pack(np.concatenate([np.pad(i["L1_ffn_sh_gate_w"], ((0, 0), (0, pad))), _flat(i["L1_ffn_gate_w"])], axis=1),
                    np.concatenate([np.pad(i["L1_ffn_sh_up_w"], ((0, 0), (0, pad))), _flat(i["L1_ffn_up_w"])], axis=1),
                    np.concatenate([np.pad(i["L1_ffn_sh_down_w"], ((0, pad), (0, 0))), i["L1_ffn_down_w"].reshape(-1, D)])),
    }


def kernel(**inputs):
    import concourse.bacc as _bacc
    from concourse.bass_utils import run_bass_kernel_spmd as _run

    nc = _bacc.Bacc("TRN2", target_bir_lowering=False, num_devices=1)
    arrays, args = {}, {}
    for name, v in _lay_out({k: np.asarray(v) for k, v in inputs.items()}).items():
        v = np.ascontiguousarray(v)
        arrays[f"in_{name}_dram"] = v
        args[name] = nc.dram_tensor(f"in_{name}_dram", v.shape, mybir.dt.from_np(v.dtype), kind="ExternalInput").ap()
    out = nc.dram_tensor("out_0_dram", (B, S, D), F32, kind="ExternalOutput").ap()
    build(nc, args, out)
    r = _run(nc, [arrays], core_ids=[0])
    return r.results[0]["out_0_dram"]
```

```python
from contextlib import ExitStack

import numpy as np

import concourse.bass as bass
from concourse import mybir
from concourse.alu_op_type import AluOpType as ALU

F32 = mybir.dt.float32
F32R = mybir.dt.float32r
BF16 = mybir.dt.bfloat16
U32 = mybir.dt.uint32
ACT = mybir.ActivationFunctionType
AX = mybir.AxisListType

P = 128
B, S, D = 8, 128, 256
T = B * S
KT = D // P
HALF = 512
NHALF = T // HALF
HB = HALF // S
A_HEADS, A_HD = 16, 8
C_HEADS, C_HD = 16, 16
TH = P // C_HD
HQ = 4
NQ = C_HEADS // HQ
TOEP = 4
EPS = 1e-5
RSQRT_MAGIC = 0x5F3759DF
MASK = -10000.0 * C_HD ** 0.5
LOWEST = -3.0e38

EXPERTS = [8, 32]
TOPK = [2, 6]
GROUPS, GSIZE, TOPG = 8, 4, 4
HID = [128, 176]
SHARED = [4, 3]
ROUTED = [E * M // P for E, M in zip(EXPERTS, HID)]
NT = [s + r for s, r in zip(SHARED, ROUTED)]
CHUNK = 16
GU = 2 * KT * P
WCOLS = GU + D


def build(nc, a, out):
    with ExitStack() as ctx:
        def sb(name, shape, dt=F32):
            return ctx.enter_context(nc.sbuf_tensor(name, shape, dt))

        def sem(name):
            return ctx.enter_context(nc.semaphore(name))

        X = sb("X", [P, B, D])
        xh = sb("xh", [P, B, D])
        xT_hi = sb("xT_hi", [P, KT, T], F32R)
        xT_lo = sb("xT_lo", [P, KT, T], F32R)
        ident = sb("ident", [P, P])
        ident_bf = sb("ident_bf", [P, P], BF16)
        gates = sb("gates", [P, 4])
        tgates = sb("tgates", [P, 4])
        bnst = sb("bnst", [P, B, 6])
        mv = sb("mv", [P, B, 2])
        rstd = sb("rstd", [P, B])
        nt1 = sb("nt1", [P, B])
        nt2 = sb("nt2", [P, B])
        magic = sb("magic", [P, B], U32)
        V = sb("V", [P, B, C_HEADS, C_HD + 1])
        KBD = sb("KBD", [P, B, KT, TH, S])
        cmask = sb("cmask", [P, HQ, S], BF16)
        lag_rows = sb("lag_rows", [A_HEADS, P + D])
        skip = sb("skip", [A_HEADS, 1])
        w_raw = sb("w_raw", [P, 2, WCOLS])
        bias1 = sb("bias1", [P, EXPERTS[1]])
        wr = [sb(f"wr{n}", [P, KT, EXPERTS[n]]) for n in range(2)]
        h_hi = [sb(f"h_hi{k}", [P, T], F32R) for k in range(2)]
        h_lo = [sb(f"h_lo{k}", [P, T], F32R) for k in range(2)]
        w_hi = [sb(f"w_hi{k}", [P, WCOLS], F32R) for k in range(2)]
        w_lo = [sb(f"w_lo{k}", [P, WCOLS], F32R) for k in range(2)]

        ARENA = 15 * 1024
        arena = sb("arena", [P, ARENA])
        at = [0]

        def take(*shape):
            n = int(np.prod(shape))
            v = arena[:, at[0]:at[0] + n]
            at[0] += n
            assert at[0] <= ARENA, at[0]
            if len(shape) == 1:
                return v
            names = "abcd"[:len(shape)]
            return v.rearrange(f"p ({' '.join(names)}) -> p {' '.join(names)}", **dict(zip(names, shape)))

        kT = take(KT, B, S)
        toep = [take(D) for _ in range(TOEP)]
        kv = [take(KT * B, A_HD, A_HD) for _ in range(2)]
        prod = [take(KT * B, A_HD, A_HD) for _ in range(2)]
        qT = take(KT, T)
        oA = take(KT * B, S)
        at[0] = 0
        sg = take(T)
        hh = take(T)
        cb = [take(T) for _ in range(2)]
        combT = take(T)
        yT = take(KT, T)
        xT = take(KT, T)
        rt = [take(B, EXPERTS[1]) for _ in range(8)]
        half_words = take(5, B, 16 + EXPERTS[1]).rearrange("p n b e -> p (n b e)").bitcast(BF16)
        counts = half_words.rearrange("p (n b e) -> p n b e", n=10, b=B)
        scan = [counts[:, n, :, :] for n in range(2)]
        ties, picked = counts[:, 2, :, 0:EXPERTS[1]], counts[:, 3, :, 0:EXPERTS[1]]
        top8 = take(B, 8)
        rs = [take(B) for _ in range(3)]
        comb = take(B, EXPERTS[1])
        gmask = take(B, GROUPS)
        at[0] = 0
        Sm = [take(HQ, S) for _ in range(2)]
        Pm = [[take(HQ, S) for _ in range(NQ)] for _ in range(2)]
        PTs = [take(HQ, S) for _ in range(2)]
        qc = [take(KT, S) for _ in range(2)]
        xr = [take(D) for _ in range(2)]
        mx = [take(HQ) for _ in range(2)]
        oC = take(C_HEADS, C_HD)
        rC = [take(C_HEADS) for _ in range(2)]

        psum = ctx.enter_context(nc.psum_tensor("psum", [P, 8, HALF], F32))
        bank = [psum[:, k, :] for k in range(8)]

        in_x = [sem(f"in_x{h}") for h in range(NHALF)]
        in_kT, in_V, in_gates, in_small, in_kbd = (sem(n) for n in
            ("in_kT", "in_V", "in_gates", "in_small", "in_kbd"))
        in_lags, lags_ready, lags_out = sem("in_lags"), sem("lags_ready"), sem("lags_out")
        in_toep = [sem(f"in_toep{k}") for k in range(TOEP)]
        pool_const, pool_kbd0, pool_v1 = sem("pool_const"), sem("pool_kbd0"), sem("pool_v1")
        dve_step = sem("dve_step")
        act_gates = sem("act_gates")
        norm_ready = sem("norm_ready")
        xt_ready = sem("xt_ready")
        xt_out = sem("xt_out")
        xlo_ready = sem("xlo_ready")
        kv_ready, conv_done, prod_ready, conv_out = (sem(n) for n in
            ("kv_ready", "conv_done", "prod_ready", "conv_out"))
        oT_ready = sem("oT_ready")
        x_new = sem("x_new")

        names = ("logits", "logits_kept", "router_in", "router_act", "comb_ready", "comb_T", "comb_copied",
                 "comb_out", "whi_gu", "whi_d", "wlo_gu", "wlo_d", "gu_done", "down_done", "silu_done",
                 "sc_done", "h_done", "hhi_done", "hlo_done", "y_bank", "y_copied", "yT_ready", "x_full")
        L = [{name: sem(f"{name}{n}") for name in names} for n in range(2)]
        w_in = [[sem(f"w_in{n}_{k}") for k in range(2)] for n in range(2)]
        c_in = [[sem(f"c_in{n}_{k}") for k in range(2)] for n in range(2)]
        (xr_ready, q_T, q_out, s_ready, mx_ready, sm_ready, exp_done, pt_ready, pt_out, pv_ready, o_out) = (
            sem(n) for n in ("xr_ready", "q_T", "q_out", "s_ready", "mx_ready", "sm_ready", "exp_done",
                             "pt_ready", "pt_out", "pv_ready", "o_out"))
        c_stats = sem("c_stats")
        out_done = sem("out_done")

        comb_dram = [nc.dram_tensor("comb_rows0", (EXPERTS[0], T), F32, kind="Internal").ap(),
                     nc.dram_tensor("comb_rows1", (ROUTED[1] * P // CHUNK, T), F32, kind="Internal").ap()]

        lag_dram = nc.dram_tensor("lag_rows_dram", (A_HEADS, P + D), F32, kind="Internal").ap()

        def over(ap, *shape):
            return ap.unsqueeze(len(ap.shape)).broadcast_to([*ap.shape, shape[0]])

        XBANK = [[2, 3], [5, 6]]
        routed_pairs = [ROUTED[n] // 2 for n in range(2)]

        block = ctx.enter_context(nc.Block())

        @block.sync
        def _(sp):
            sp.dma_start(lag_rows[:, P:], a["lags"]).then_inc(in_lags, 16)
            sp.dma_start(skip[:], a["skip"].unsqueeze(1)).then_inc(in_lags, 16)
            sp.dma_start(kT, a["ctx_T_rev"]).then_inc(in_kT, 16)
            sp.wait_ge(lags_ready, 2)
            sp.dma_start(lag_dram, lag_rows[:]).then_inc(lags_out, 16)
            sp.wait_ge(lags_out, 16)
            toeplitz = bass.AP(lag_dram.tensor, lag_dram.offset + 1, [[1, P], [P + D, A_HEADS], [1, D]])

            def load_toep(h, k):
                sp.dma_start(toep[k], toeplitz[:, bass.ds(h, 1), :].rearrange("p o l -> p (o l)")).then_inc(in_toep[k], 16)

            for k in range(TOEP):
                load_toep(k, k)
            with sp.Fori(1, A_HEADS // TOEP) as i:
                for k in range(TOEP):
                    sp.wait_ge(conv_done, TOEP * i + (k + 1 - TOEP))
                    load_toep(TOEP * i + k, k)
            sp.wait_ge(pool_kbd0, 1)
            for h in range(TH):
                rows = slice(h * C_HD, (h + 1) * C_HD)
                for t in range(KT):
                    sp.dma_start(KBD[rows, :, t, h, :], a["ctx_T"][t, rows]).then_inc(in_kbd, 16)

            def expert_loads(n):
                q, R = L[n], ROUTED[n]

                def weights(t, k):
                    sp.wait_ge(q["wlo_d"], t + 1)
                    sp.dma_start(w_raw[:, k, :], a[f"w{n}"][t + 2]).then_inc(w_in[n][k], 16)

                def combine(r, k):
                    if n == 0:
                        src = comb_dram[0][r].unsqueeze(0).broadcast_to([P, T])
                        sp.dma_start(cb[k], src).then_inc(c_in[n][k], 16)
                    else:
                        c = P // CHUNK
                        src = comb_dram[1][bass.ds(r * c, c), :].unsqueeze(1).broadcast_to([c, CHUNK, T])
                        sp.dma_start(cb[k], src).then_inc(c_in[n][k], 16)

                for t in range(2):
                    weights(t, t)
                sp.wait_ge(q["comb_copied"], 2)
                if n == 0:
                    sp.dma_start(comb_dram[0], combT[0:EXPERTS[0], :]).then_inc(q["comb_out"], 16)
                else:
                    rep = HID[1] // CHUNK
                    sp.dma_start(comb_dram[1].rearrange("(e c) t -> e c t", c=rep),
                                 combT[0:EXPERTS[1], :].unsqueeze(1).broadcast_to([EXPERTS[1], rep, T])
                                 ).then_inc(q["comb_out"], 16)
                weights(2, 0)
                sp.wait_ge(q["comb_out"], 16)
                for k in range(2):
                    combine(k, k)
                for t in range(3, SHARED[n]):
                    weights(t, t % 2)
                with sp.Fori(0, routed_pairs[n] - 1) as i:
                    for k in range(2):
                        t = 2 * i + (SHARED[n] + k)
                        weights(t, (SHARED[n] + k) % 2)
                        sp.wait_ge(q["sc_done"], 4 * i + 2 * (k + 1))
                        combine(2 * i + (k + 2), k)

            expert_loads(0)
            sp.wait_ge(L[0]["wlo_d"], NT[0])
            for k in range(2):
                sp.dma_start(w_raw[:, k, :], a["w1"][k]).then_inc(w_in[1][k], 16)
            expert_loads(1)
            for q in range(B // 2):
                sp.wait_ge(x_new, 8 + q + 1)
                sp.dma_start(out[2 * q:2 * q + 2].rearrange("b s d -> s b d"), X[:, 2 * q:2 * q + 2, :]).then_inc(out_done, 16)
            sp.wait_ge(out_done, 16 * (B // 2))

        @block.gpsimd
        def _(pool):
            def diagonal(m, n):
                pool.memset(m[:], 0.0).then_inc(pool_const, 1)
                pool.wait_ge(pool_const, n)
                pool.affine_select(out=m[:], in_=m[:], compare_op=ALU.not_equal, fill=1.0,
                                   base=0, pattern=[[-1, P]], channel_multiplier=1).then_inc(pool_const, 1)

            diagonal(ident, 1)

            kT3 = kT.rearrange("p t b s -> p (t b) s")

            def key_value(h, k, first):
                if not first:
                    pool.wait_ge(conv_done, h - 1)
                src = kT3[:, :, bass.ds(h * A_HD, A_HD)]
                pool.tensor_tensor(kv[k], src.unsqueeze(3).broadcast_to([P, KT * B, A_HD, A_HD]),
                                   src.unsqueeze(2).broadcast_to([P, KT * B, A_HD, A_HD]), ALU.mult).then_inc(kv_ready, 1)

            pool.wait_ge(in_kT, 16)
            for k in range(2):
                key_value(k, k, True)
            with pool.Fori(1, A_HEADS // 2) as i:
                for k in range(2):
                    key_value(2 * i + k, k, False)
            diagonal(ident_bf, 3)
            pool.memset(cmask[:], 0.0).then_inc(pool_const, 1)
            pool.wait_ge(pool_const, 5)
            pool.affine_select(out=cmask[:], in_=cmask[:], compare_op=ALU.is_ge, fill=MASK,
                               base=0, pattern=[[0, HQ], [-1, S]], channel_multiplier=1).then_inc(pool_const, 1)
            pool.memset(KBD[:], 0.0).then_inc(pool_kbd0, 1)
            pool.wait_ge(in_V, 16)
            pool.memset(V[:, :, :, C_HD:], 1.0).then_inc(pool_v1, 1)

        @block.scalar
        def _(act):
            for h in range(NHALF):
                act.dma_start(X[:, h * HB:(h + 1) * HB, :],
                              a["x"][h * HB:(h + 1) * HB].rearrange("b s d -> s b d")).then_inc(in_x[h], 16)
            act.dma_start(gates[:], a["gates"].unsqueeze(0).broadcast_to([P, 4])).then_inc(in_gates, 16)
            for k in range(2):
                act.dma_start(w_raw[:, k, :], a["w0"][k]).then_inc(w_in[0][k], 16)
            for n in range(2):
                act.dma_start(wr[n][:], a[f"wr{n}"]).then_inc(in_small, 16)
            act.dma_start(bias1[:], a["bias1"].unsqueeze(0).broadcast_to([P, EXPERTS[1]])).then_inc(in_small, 16)
            act.dma_start(V[:], a["ctx_v"]).then_inc(in_V, 16)
            act.wait_ge(in_gates, 16)
            act.activation(tgates[:], gates[:], ACT.Tanh).then_inc(act_gates, 1)

            for n, (h, t) in enumerate((h, t) for h in range(2) for t in range(KT)):
                act.wait_ge(xt_ready, n + 1)
                act.copy(qT[:, t, h * HALF:(h + 1) * HALF], bank[2 * t + h]).then_inc(xt_out, 1)
            def experts(n, transposed):
                q, S0, N = L[n], SHARED[n], NT[n]

                def split_gu(t, k, landed=None):
                    act.wait_ge(w_in[n][k], 16 * (t // 2 + 1) if landed is None else landed)
                    if not (isinstance(t, int) and t < 2):
                        act.wait_ge(q["gu_done"], 2 * t - 2)
                    act.copy(w_hi[k][:, :GU], w_raw[:, k, :GU]).then_inc(q["whi_gu"], 1)

                def step(t, k, landed=None, last=False):
                    if not last:
                        split_gu(t + 1, 1 - k, landed)
                    if not (isinstance(t, int) and t < 2):
                        act.wait_ge(q["down_done"], t - 1)
                    act.copy(w_hi[k][:, GU:], w_raw[:, k, GU:]).then_inc(q["whi_d"], 1)
                    for h in range(NHALF):
                        act.wait_ge(q["gu_done"], 2 * t + (h + 1))
                        act.activation(sg[:, h * HALF:(h + 1) * HALF], bank[2 * h], ACT.Silu).then_inc(q["silu_done"], 1)
                    for h in range(NHALF):
                        cols = slice(h * HALF, (h + 1) * HALF)
                        act.wait_ge(q["h_done"], 2 * t + (h + 1))
                        act.copy(h_hi[k][:, cols], hh[:, cols]).then_inc(q["hhi_done"], 1)

                split_gu(0, 0)
                for h in range(NHALF):
                    cols = slice(h * HALF, (h + 1) * HALF)
                    for t in range(KT):
                        act.wait_ge(xt_ready, 4 * transposed + KT * h + t + 1)
                        act.copy(xT[:, t, cols], bank[XBANK[h][t]]).then_inc(q["x_full"], 1)
                    for t in range(KT):
                        act.wait_ge(q["x_full"], KT * h + t + 1)
                        act.copy(xT_hi[:, t, cols], xT[:, t, cols]).then_inc(xt_out, 1)
                E = EXPERTS[n]
                if n == 0:
                    act.wait_ge(q["router_in"], 1)
                    act.activation(rt[1][:, :, 0:E], rt[0][:, :, 0:E], ACT.Exp).then_inc(q["router_act"], 1)
                else:
                    act.wait_ge(q["logits"], 1)
                    act.activation(rt[1][:, :, 0:E], bank[4][:, 0:B * E].rearrange("p (b e) -> p b e", b=B),
                                   ACT.Sigmoid).then_inc(q["logits_kept"], 1)
                for t in range(3):
                    step(t, t % 2)
                for h in range(NHALF):
                    act.wait_ge(q["comb_T"], h + 1)
                    act.copy(combT[0:E, h * HALF:(h + 1) * HALF], bank[h][0:E, :]).then_inc(q["comb_copied"], 1)
                for t in range(3, S0):
                    step(t, t % 2)
                with act.Fori(0, routed_pairs[n] - 1) as i:
                    for k in range(2):
                        step(2 * i + (S0 + k), (S0 + k) % 2, 16 * i + 16 * ((S0 + k + 1) // 2 + 1))
                step(N - 2, N % 2)
                step(N - 1, (N - 1) % 2, last=True)
                for h in range(NHALF):
                    for t in range(KT):
                        act.wait_ge(q["y_bank"], KT * h + t + 1)
                        act.copy(yT[:, t, h * HALF:(h + 1) * HALF], bank[4 + 2 * t + h]).then_inc(q["y_copied"], 1)

            experts(0, 1)

            def queries(b, k):
                act.wait_ge(q_T, b + 1)
                act.copy(qc[k], bank[6][:, 0:D].rearrange("p (t s) -> p t s", t=KT)).then_inc(q_out, 1)

            def exponentials(b, k, j):
                act.wait_ge(sm_ready, NQ * b + (j + 1))
                act.activation(Pm[k][j], Sm[j % 2], ACT.Exp, scale=C_HD ** -0.5).then_inc(exp_done, 1)

            def attend(b, k, last=False, ahead=True):
                for j in range(NQ):
                    act.wait_ge(pt_ready, NQ * b + (j + 1))
                    act.copy(PTs[j % 2], bank[4 + j % 2].rearrange("p (h s) -> p h s", h=HQ)).then_inc(pt_out, 1)
                    if not last:
                        exponentials(b + 1, 1 - k, j)
                    if j == 1 and ahead:
                        queries(b + 2, k)

            for b in range(2):
                queries(b, b)
            for j in range(NQ):
                exponentials(0, 0, j)
            attend(0, 0)
            with act.Fori(0, 2) as i:
                for k in range(2):
                    attend(2 * i + (1 + k), (1 + k) % 2)
            attend(5, 1)
            attend(6, 0, ahead=False)
            attend(7, 1, last=True, ahead=False)

            experts(1, 2)

        @block.vector
        def _(dve):
            class Chain:
                def __init__(self):
                    self.n = 0

                def add(self, ins):
                    ins.then_inc(dve_step, 1)
                    self.n += 1

                def wait(self):
                    dve.wait_ge(dve_step, self.n)

                def link(self, ins):
                    self.add(ins)
                    self.wait()

            chain = Chain()
            link = chain.link
            link(dve.memset(magic[:], RSQRT_MAGIC + 1))

            def statistics():
                for b in range(B):
                    chain.add(dve.bn_aggr(mv[:, b, :], bnst[:, b, :]))
                chain.wait()
                link(dve.tensor_scalar(nt2[:], mv[:, :, 1], EPS, None, ALU.add))
                link(dve.tensor_scalar(nt1[:].bitcast(U32), nt2[:].bitcast(U32), 1, 0xFFFFFFFF,
                                       ALU.logical_shift_right, ALU.bitwise_xor))
                link(dve.tensor_tensor(rstd[:].bitcast(U32), nt1[:].bitcast(U32), magic[:], ALU.add))
                for _ in range(3):
                    link(dve.scalar_tensor_tensor(out=nt1[:], in0=rstd[:], scalar=-0.5, in1=rstd[:], op0=ALU.mult, op1=ALU.mult))
                    link(dve.tensor_tensor(nt1[:], nt1[:], nt2[:], ALU.mult))
                    link(dve.scalar_tensor_tensor(out=rstd[:], in0=nt1[:], scalar=1.5, in1=rstd[:], op0=ALU.add, op1=ALU.mult))

            def batch_statistics(b):
                chain.add(dve.bn_stats(bnst[:, b, :], X[:, b, :]))

            def norm_rows(b0, b1):
                for b in range(b0, b1):
                    dve.tensor_scalar(xh[:, b, :], X[:, b, :], mv[:, b, 0:1], rstd[:, b:b + 1],
                                      ALU.subtract, ALU.mult).then_inc(norm_ready, 1)

            q3 = qT.rearrange("p t (b s) -> p (t b) s", b=B)

            def weigh(h, k, first=False):
                dve.wait_ge(conv_done, h + 1)
                if not first:
                    dve.wait_ge(conv_out, h - 1)
                y = psum[:, 4 + 2 * k:6 + 2 * k, :].rearrange("p t (b j i) -> p (t b) j i", b=B, j=A_HD)
                q = q3[:, :, bass.ds(h * A_HD, A_HD)].unsqueeze(2).broadcast_to([P, KT * B, A_HD, A_HD])
                dve.tensor_tensor(prod[k], y, q, ALU.mult).then_inc(prod_ready, 1)

            def reduce(h, k):
                dve.wait_ge(prod_ready, h + 1)
                dve.tensor_reduce(oA[:, :, bass.ds(h * A_HD, A_HD)], prod[k], AX.X, ALU.add).then_inc(conv_out, 1)

            dve.memset(lag_rows[:, 0:P], 0.0).then_inc(lags_ready, 1)
            dve.wait_ge(in_lags, 32)
            dve.tensor_tensor(lag_rows[:, P:P + 1], lag_rows[:, P:P + 1], skip[:], ALU.add).then_inc(lags_ready, 1)
            for b in range(B):
                if b % HB == 0:
                    dve.wait_ge(in_x[b // HB], 16)
                batch_statistics(b)
            chain.wait()
            statistics()
            norm_rows(0, B)
            dve.wait_ge(xt_out, 4)
            for k in range(2):
                weigh(k, k, first=True)
            reduce(0, 0)
            with dve.Fori(0, A_HEADS // 2 - 1) as i:
                for k in range(2):
                    weigh(2 * i + (2 + k), k)
                    reduce(2 * i + (1 + k), 1 - k)
            reduce(A_HEADS - 1, 1)

            def add_banks(ready, gate, before):
                for q in range(B // 2):
                    dve.wait_ge(ready, q + 1)
                    rows = X[:, 2 * q:2 * q + 2, :].rearrange("p b d -> p (b d)")
                    dve.scalar_tensor_tensor(out=rows, in0=bank[q], scalar=tgates[:, gate:gate + 1], in1=rows,
                                             op0=ALU.mult, op1=ALU.add).then_inc(x_new, 1)
                    if before < 8:
                        dve.wait_ge(x_new, before + q + 1)
                        for b in (2 * q, 2 * q + 1):
                            batch_statistics(b)
                chain.wait()

            def top_mask(v, E, K, sel):
                for b in range(B):
                    chain.add(dve.max(out=top8[:, b, :], in_=v[:, b, :]))
                chain.wait()
                kth = top8[:, :, K - 1:K].broadcast_to([P, B, E])
                above, tied = picked[:, :, 0:E], ties[:, :, 0:E]
                chain.add(dve.tensor_tensor(above, v, kth, ALU.is_gt))
                chain.add(dve.tensor_tensor(tied, v, kth, ALU.is_equal))
                chain.wait()
                chain.add(dve.tensor_reduce(rs[0], above, AX.X, ALU.add))
                cur, shift = 0, 1
                first = scan[0][:, :, 16:16 + E]
                chain.add(dve.tensor_copy(first, tied))
                chain.wait()
                chain.add(dve.tensor_scalar(rs[1], rs[0], -1.0, float(K), ALU.mult, ALU.add))
                while shift < E:
                    link(dve.tensor_tensor(scan[1 - cur][:, :, 16:16 + E], scan[cur][:, :, 16:16 + E],
                                           scan[cur][:, :, 16 - shift:16 - shift + E], ALU.add))
                    cur, shift = 1 - cur, 2 * shift
                link(dve.tensor_tensor(scan[1 - cur][:, :, 16:16 + E], scan[cur][:, :, 16:16 + E], over(rs[1], E), ALU.is_le))
                link(dve.tensor_tensor(tied, tied, scan[1 - cur][:, :, 16:16 + E], ALU.mult))
                link(dve.tensor_tensor(sel, above, tied, ALU.add))

            def softmax_in(q, E):
                logits = bank[4][:, 0:B * E].rearrange("p (b e) -> p b e", b=B)
                dve.wait_ge(q["logits"], 1)
                link(dve.tensor_reduce(rs[0], logits, AX.X, ALU.max))
                dve.tensor_tensor(rt[0][:, :, 0:E], logits, over(rs[0], E), ALU.subtract).then_inc(q["router_in"], 1)

            def route0(q):
                E, K = EXPERTS[0], TOPK[0]
                e, p, sel, c = (rt[k][:, :, 0:E] for k in (1, 2, 3, 4))
                dve.wait_ge(q["router_act"], 1)
                link(dve.tensor_reduce(rs[0], e, AX.X, ALU.add))
                link(dve.reciprocal(rs[1], rs[0]))
                link(dve.tensor_tensor(p, e, over(rs[1], E), ALU.mult))
                top_mask(p, E, K, sel)
                link(dve.tensor_tensor(c, p, sel, ALU.mult))
                link(dve.tensor_reduce(rs[0], c, AX.X, ALU.add))
                link(dve.reciprocal(rs[1], rs[0]))
                dve.tensor_tensor(comb[:, :, 0:E], c, over(rs[1], E), ALU.mult).then_inc(q["comb_ready"], 1)

            def groups1(q):
                E = EXPERTS[1]
                score, sfc = rt[1], rt[2]
                dve.wait_ge(q["logits_kept"], 1)
                link(dve.tensor_tensor(sfc, score, bias1[:].unsqueeze(1).broadcast_to([P, B, E]), ALU.add))
                pair = sfc.rearrange("p b (x y) -> p (b x) y", y=2)
                hi2, lo2 = (rt[k].rearrange("p b e -> p (b e)")[:, 0:B * GROUPS * 2] for k in (4, 5))
                chain.add(dve.tensor_tensor(hi2, pair[:, :, 0], pair[:, :, 1], ALU.max))
                chain.add(dve.tensor_tensor(lo2, pair[:, :, 0], pair[:, :, 1], ALU.min))
                chain.wait()
                hi2, lo2 = (v.rearrange("p (g y) -> p g y", y=2) for v in (hi2, lo2))
                t1, t2, t3 = (rt[k].rearrange("p b e -> p (b e)")[:, B * GROUPS * 2:B * GROUPS * 3] for k in (4, 5, 6))
                gs = rt[6].rearrange("p b e -> p (b e)")[:, 0:B * GROUPS]
                chain.add(dve.tensor_tensor(t1, hi2[:, :, 0], hi2[:, :, 1], ALU.max))
                chain.add(dve.tensor_tensor(t2, hi2[:, :, 0], hi2[:, :, 1], ALU.min))
                chain.add(dve.tensor_tensor(t3, lo2[:, :, 0], lo2[:, :, 1], ALU.max))
                chain.wait()
                link(dve.tensor_tensor(t2, t2, t3, ALU.max))
                link(dve.tensor_tensor(gs, t1, t2, ALU.add))
                top_mask(gs.rearrange("p (b g) -> p b g", b=B), GROUPS, TOPG, gmask)
                fill = rt[4].rearrange("p b e -> p (b e)")[:, 0:B * GROUPS]
                gm = gmask.rearrange("p b g -> p (b g)")
                link(dve.tensor_scalar(fill, gm, 1.0, -LOWEST, ALU.subtract, ALU.mult))
                s4 = sfc.rearrange("p b (g e) -> p (b g) e", e=GSIZE)
                link(dve.tensor_tensor(s4, s4, over(gm, GSIZE), ALU.mult))
                link(dve.tensor_tensor(s4, s4, over(fill, GSIZE), ALU.add))

            def route1(q):
                score, sfc, sel = rt[1], rt[2], rt[3]
                top_mask(sfc, EXPERTS[1], TOPK[1], sel)
                dve.tensor_tensor(comb, score, sel, ALU.mult).then_inc(q["comb_ready"], 1)

            def experts(n, transposed):
                q, S0, N = L[n], SHARED[n], NT[n]

                def split_gu(t, k):
                    dve.wait_ge(q["whi_gu"], t + 1)
                    dve.tensor_tensor(w_lo[k][:, :GU], w_raw[:, k, :GU], w_hi[k][:, :GU].bitcast(F32),
                                      ALU.subtract).then_inc(q["wlo_gu"], 1)

                def step(t, k, r=None, last=False):
                    if not last:
                        split_gu(t + 1, 1 - k)
                    dve.wait_ge(q["whi_d"], t + 1)
                    dve.tensor_tensor(w_lo[k][:, GU:], w_raw[:, k, GU:], w_hi[k][:, GU:].bitcast(F32),
                                      ALU.subtract).then_inc(q["wlo_d"], 1)
                    for h in range(NHALF):
                        cols = slice(h * HALF, (h + 1) * HALF)
                        dve.wait_ge(q["silu_done"], 2 * t + (h + 1))
                        if not isinstance(t, int) or t > 0:
                            dve.wait_ge(q["hlo_done"], 2 * t + (h - 1))
                        if r is None:
                            dve.tensor_tensor(hh[:, cols], sg[:, cols], bank[2 * h + 1], ALU.mult).then_inc(q["h_done"], 1)
                        else:
                            index, slot, landed = r
                            if h == 0:
                                dve.wait_ge(c_in[n][slot], landed)
                            dve.tensor_tensor(hh[:, cols], sg[:, cols], cb[slot][:, cols], ALU.mult).then_inc(q["sc_done"], 1)
                            dve.wait_ge(q["sc_done"], 2 * index + (h + 1))
                            dve.tensor_tensor(hh[:, cols], hh[:, cols], bank[2 * h + 1], ALU.mult).then_inc(q["h_done"], 1)
                    for h in range(NHALF):
                        cols = slice(h * HALF, (h + 1) * HALF)
                        dve.wait_ge(q["hhi_done"], 2 * t + (h + 1))
                        dve.tensor_tensor(h_lo[k][:, cols], hh[:, cols], h_hi[k][:, cols].bitcast(F32),
                                          ALU.subtract).then_inc(q["hlo_done"], 1)

                def low(h):
                    for t in range(KT):
                        cols = slice(h * HALF, (h + 1) * HALF)
                        dve.wait_ge(xt_out, 4 * transposed + KT * h + t + 1)
                        dve.tensor_tensor(xT_lo[:, t, cols], xT[:, t, cols], xT_hi[:, t, cols].bitcast(F32),
                                          ALU.subtract).then_inc(xlo_ready, 1)

                statistics()
                norm_rows(0, 6)
                low(0)
                norm_rows(6, B)
                low(1)
                if n == 0:
                    softmax_in(q, EXPERTS[0])
                else:
                    groups1(q)
                step(0, 0)
                step(1, 1)
                (route0 if n == 0 else route1)(q)
                for t in range(2, S0):
                    step(t, t % 2)
                with dve.Fori(0, routed_pairs[n] - 1) as i:
                    for k in range(2):
                        step(2 * i + (S0 + k), (S0 + k) % 2, (2 * i + k, k, 16 * i + 16))
                for k in range(2):
                    step(N - 2 + k, (N + k) % 2, (ROUTED[n] - 2 + k, k, 16 * routed_pairs[n]), last=k == 1)

            def split_first(n):
                dve.wait_ge(L[n]["whi_gu"], 1)
                dve.tensor_tensor(w_lo[0][:, :GU], w_raw[:, 0, :GU], w_hi[0][:, :GU].bitcast(F32),
                                  ALU.subtract).then_inc(L[n]["wlo_gu"], 1)

            split_first(0)
            for c in counts[:, 0, :, 0:16], counts[:, 1, :, 0:16]:
                chain.add(dve.memset(c, 0.0))
            dve.wait_ge(act_gates, 1)
            add_banks(oT_ready, 0, 0)
            experts(0, 1)
            add_banks(L[0]["yT_ready"], 2, 4)

            def normed(b, k):
                dve.tensor_scalar(xr[k], X[:, bass.ds(b, 1), :].rearrange("p o d -> p (o d)"), mv[:, bass.ds(b, 1), 0:1].rearrange("p o c -> p (o c)"), rstd[:, bass.ds(b, 1)],
                                  ALU.subtract, ALU.mult).then_inc(xr_ready, 1)

            def less_maximum(b, j, first=False):
                scores = bank[j].rearrange("p (h s) -> p h s", h=HQ)
                dve.wait_ge(s_ready, NQ * b + (j + 1))
                dve.tensor_reduce(mx[j % 2], scores, AX.X, ALU.max).then_inc(mx_ready, 1)
                dve.wait_ge(mx_ready, NQ * b + (j + 1))
                if not (first and j < 2):
                    dve.wait_ge(exp_done, NQ * b + (j - 1))
                dve.tensor_tensor(Sm[j % 2], scores, over(mx[j % 2], S), ALU.subtract).then_inc(sm_ready, 1)

            def add_heads(b):
                o = bank[7][:, 0:C_HEADS * (C_HD + 1)].rearrange("p (h c) -> p h c", h=C_HEADS)
                dve.wait_ge(pv_ready, b + 1)
                dve.reciprocal(rC[0], o[:, :, C_HD]).then_inc(o_out, 1)
                dve.wait_ge(o_out, 4 * b + 1)
                dve.tensor_scalar(rC[1], rC[0], tgates[:, 1:2], None, ALU.mult).then_inc(o_out, 1)
                dve.wait_ge(o_out, 4 * b + 2)
                dve.tensor_tensor(oC, o[:, :, 0:C_HD], over(rC[1], C_HD), ALU.mult).then_inc(o_out, 1)
                dve.wait_ge(o_out, 4 * b + 3)
                xb = X[:, bass.ds(b, 1), :].rearrange("p o d -> p (o d)")
                dve.tensor_tensor(xb, xb, oC.rearrange("p h c -> p (h c)"), ALU.add).then_inc(o_out, 1)
                dve.wait_ge(o_out, 4 * b + 4)
                dve.bn_stats(bnst[:, bass.ds(b, 1), :].rearrange("p o c -> p (o c)"), xb).then_inc(c_stats, 1)

            statistics()
            for b in range(2):
                normed(b, b)
            for j in range(NQ):
                less_maximum(0, j, first=True)

            def attend(b, k, first=False, last=False, ahead=True):
                if ahead:
                    dve.wait_ge(q_out, b + 1)
                    normed(b + 2, k)
                for j in range(NQ):
                    if not last:
                        less_maximum(b + 1, j)
                    if j == 0 and not first:
                        add_heads(b - 1)

            attend(0, 0, first=True)
            with dve.Fori(0, 2) as i:
                for k in range(2):
                    attend(2 * i + (1 + k), (1 + k) % 2)
            attend(5, 1)
            attend(6, 0, ahead=False)
            attend(7, 1, last=True, ahead=False)
            split_first(1)
            for c in counts[:, 0, :, 0:16], counts[:, 1, :, 0:16]:
                chain.add(dve.memset(c, 0.0))
            add_heads(7)
            dve.wait_ge(c_stats, B)
            experts(1, 2)
            add_banks(L[1]["yT_ready"], 3, 8)

        @block.tensor
        def _(pe):
            def transpose_norm(n, banks):
                for h in range(NHALF):
                    for t in range(KT):
                        for b in range(h * HB, (h + 1) * HB):
                            pe.wait_ge(norm_ready, B * n + b + 1)
                            c = (b - h * HB) * S
                            mm = pe.transpose(bank[banks[h][t]][:, c:c + S], xh[:, b, t * P:(t + 1) * P], ident[:])
                        mm.then_inc(xt_ready, 1)

            def convolve(h, slot, landed, first=False):
                k = slot % 2
                pe.wait_ge(kv_ready, h + 1)
                pe.wait_ge(in_toep[slot], landed)
                if not first:
                    pe.wait_ge(prod_ready, h - 1)
                near, far = toep[slot][:, 0:P], toep[slot][:, P:D]
                kv0, kv1 = (kv[k][:, t * B:(t + 1) * B].rearrange("p b j i -> p (b j i)") for t in range(KT))
                pe.matmul(bank[4 + 2 * k], near, kv0, start=True, stop=True)
                pe.matmul(bank[5 + 2 * k], far, kv0, start=True, stop=False)
                pe.matmul(bank[5 + 2 * k], near, kv1, start=False, stop=True).then_inc(conv_done, 1)

            for k in range(2):
                convolve(k, k, 16, first=True)
            pe.wait_ge(pool_const, 2)
            transpose_norm(0, [[0, 2], [1, 3]])
            for k in range(2, TOEP):
                convolve(k, k, 16)
            with pe.Fori(1, A_HEADS // TOEP) as i:
                for k in range(TOEP):
                    convolve(TOEP * i + k, k, 16 * i + 16)
            pe.wait_ge(conv_out, A_HEADS)
            for q in range(B // 2):
                for b in (2 * q, 2 * q + 1):
                    for t in range(KT):
                        c = (b % 2) * D + t * P
                        mm = pe.transpose(bank[q][:, c:c + P], oA[:, t * B + b, :], ident[:])
                mm.then_inc(oT_ready, 1)

            def experts(n, norm, transposed):
                q, S0, N, E = L[n], SHARED[n], NT[n], EXPERTS[n]
                transpose_norm(norm, XBANK)

                def gate_up(t, k, first=False):
                    pe.wait_ge(q["wlo_gu"], t + 1)
                    for h in range(NHALF):
                        if first:
                            pe.wait_ge(xlo_ready, 4 * (transposed - 1) + KT * (h + 1))
                        else:
                            pe.wait_ge(q["silu_done"], 2 * t + (h - 1))
                            pe.wait_ge(q["h_done"], 2 * t + (h - 1))
                        x = slice(h * HALF, (h + 1) * HALF)
                        for g in range(2):
                            m = 0
                            for c in range(KT):
                                w = slice((g * KT + c) * P, (g * KT + c + 1) * P)
                                for wp, xp in ((w_hi[k], xT_hi), (w_hi[k], xT_lo), (w_lo[k], xT_hi)):
                                    mm = pe.matmul(bank[2 * h + g], wp[:, w], xp[:, c, x], start=m == 0, stop=m == 3 * KT - 1)
                                    m += 1
                        mm.then_inc(q["gu_done"], 1)

                def down(t, k, first=False, last=False):
                    pe.wait_ge(q["wlo_d"], t + 1)
                    for h in range(NHALF):
                        pe.wait_ge(q["hlo_done"], 2 * t + (h + 1))
                        x = slice(h * HALF, (h + 1) * HALF)
                        for c in range(KT):
                            w = slice(GU + c * P, GU + (c + 1) * P)
                            for m, (wp, hp) in enumerate(((w_hi[k], h_hi[k]), (w_hi[k], h_lo[k]), (w_lo[k], h_hi[k]))):
                                mm = pe.matmul(bank[4 + 2 * c + h], wp[:, w], hp[:, x], start=first and m == 0,
                                               stop=last and m == 2, skip_group_check=True)
                            if last:
                                mm.then_inc(q["y_bank"], 1)
                    if not last:
                        mm.then_inc(q["down_done"], 1)

                pe.wait_ge(in_small, 48)
                for b in range(B):
                    pe.wait_ge(q["x_full"], KT * (b // HB + 1))
                    for c in range(KT):
                        mm = pe.matmul(bank[4][:, b * E:(b + 1) * E], xT[:, c, b * S:(b + 1) * S], wr[n][:, c, :],
                                       start=c == 0, stop=c == KT - 1)
                mm.then_inc(q["logits"], 1)
                gate_up(0, 0, first=True)
                gate_up(1, 1)
                pe.wait_ge(q["router_in" if n == 0 else "logits_kept"], 1)
                down(0, 0, first=True)
                gate_up(2, 0)
                down(1, 1)
                pe.wait_ge(q["comb_ready"], 1)
                pe.wait_ge(q["silu_done"], 5)
                pe.wait_ge(q["h_done"], 5)
                for h in range(NHALF):
                    for b in range(h * HB, (h + 1) * HB):
                        c = (b - h * HB) * S
                        mm = pe.transpose(bank[h][0:E, c:c + S], comb[:, b, 0:E], ident[:])
                    mm.then_inc(q["comb_T"], 1)
                pe.wait_ge(q["comb_copied"], 2)
                for t in range(3, S0):
                    gate_up(t, t % 2)
                    down(t - 1, (t - 1) % 2)
                with pe.Fori(0, routed_pairs[n] - 1) as i:
                    for k in range(2):
                        gate_up(2 * i + (S0 + k), (S0 + k) % 2)
                        down(2 * i + (S0 + k - 1), (S0 + k - 1) % 2)
                for t in range(N - 2, N):
                    gate_up(t, t % 2)
                    down(t - 1, (t - 1) % 2)
                down(N - 1, (N - 1) % 2, last=True)
                for p in range(B // 2):
                    pe.wait_ge(q["y_copied"], KT * (2 * p // HB + 1))
                    for b in (2 * p, 2 * p + 1):
                        for t in range(KT):
                            c = (b % 2) * D + t * P
                            mm = pe.transpose(bank[p][:, c:c + P], yT[:, t, b * S:(b + 1) * S], ident[:])
                    mm.then_inc(q["yT_ready"], 1)

            experts(0, 1, 1)

            def queries(b, k):
                pe.wait_ge(xr_ready, b + 1)
                if not isinstance(b, int) or b > 0:
                    pe.wait_ge(q_out, b)
                for t in range(KT):
                    mm = pe.transpose(bank[6][:, t * S:(t + 1) * S], xr[k][:, t * P:(t + 1) * P], ident[:])
                mm.then_inc(q_T, 1)

            def scores(b, k, j, first=False):
                if j == 0:
                    pe.wait_ge(q_out, b + 1)
                if not first:
                    pe.wait_ge(sm_ready, NQ * b + (j + 1 - NQ))
                t, h = j // (NQ // KT), HQ * (j % (NQ // KT))
                pe.matmul(bank[j], ident_bf[:], cmask[:].rearrange("p h s -> p (h s)"), start=True, stop=False)
                pe.matmul(bank[j], qc[k][:, t, :], KBD[:, bass.ds(b, 1), t, h:h + HQ, :].rearrange("p o h s -> p (o h s)"),
                          start=False, stop=True).then_inc(s_ready, 1)

            def values(b, j, wait_out=True):
                pe.wait_ge(pt_out, NQ * b + (j + 1))
                if j == 0 and wait_out:
                    pe.wait_ge(o_out, 4 * b - 1)
                for h in range(HQ):
                    head = HQ * j + h
                    c = head * (C_HD + 1)
                    mm = pe.matmul(bank[7][:, c:c + C_HD + 1], PTs[j % 2][:, h, :],
                                   V[:, bass.ds(b, 1), head, :].rearrange("p o c -> p (o c)"), start=True, stop=True)
                if j == NQ - 1:
                    mm.then_inc(pv_ready, 1)

            def attend(b, k, first=False, last=False, ahead=True):
                for j in range(NQ):
                    if not last:
                        scores(b + 1, 1 - k, j)
                    pe.wait_ge(exp_done, NQ * b + (j + 1))
                    if not (first and j < 2):
                        pe.wait_ge(pt_out, NQ * b + (j - 1))
                    for h in range(HQ):
                        mm = pe.transpose(bank[4 + j % 2][:, h * S:(h + 1) * S], Pm[k][j][:, h, :], ident[:])
                    mm.then_inc(pt_ready, 1)
                    if j == 1 and ahead:
                        queries(b + 2, k)
                    if j > 0:
                        values(b, j - 1, wait_out=not first)
                    elif not first:
                        values(b - 1, NQ - 1)

            pe.wait_ge(pool_v1, 1)
            pe.wait_ge(pool_const, 6)
            pe.wait_ge(in_kbd, 16 * TH * KT)
            for b in range(2):
                queries(b, b)
            for j in range(NQ):
                scores(0, 0, j, first=True)
            attend(0, 0, first=True)
            with pe.Fori(0, 2) as i:
                for k in range(2):
                    attend(2 * i + (1 + k), (1 + k) % 2)
            attend(5, 1)
            attend(6, 0, ahead=False)
            attend(7, 1, last=True, ahead=False)
            values(7, NQ - 1)

            experts(1, 2, 2)


def _pack(gate, up, down):
    n = gate.shape[1] // P
    g, u = (w.reshape(KT, P, n, P).transpose(2, 1, 0, 3).reshape(n, P, KT * P) for w in (gate, up))
    return np.concatenate([g, u, down.reshape(n, P, D)], axis=2)


def _flat(w):
    return w.transpose(1, 0, 2).reshape(D, -1)


def _lay_out(i):
    pad = SHARED[1] * P - i["L1_ffn_sh_gate_w"].shape[1]
    ctx_T = np.ascontiguousarray(i["ctx_2048"].transpose(2, 0, 1)).reshape(KT, P, B, S)
    gu0, sgu0 = i["L0_ffn_w_gate_up"], i["L0_ffn_w_sh_gate_up"]
    m0, sh0 = HID[0], SHARED[0] * P
    ctx_v = np.ones((S, B, C_HEADS, C_HD + 1), np.float32)
    ctx_v[..., :C_HD] = i["ctx_2048"].transpose(1, 0, 2).reshape(S, B, C_HEADS, C_HD)
    return {
        "x": i["x"],
        "ctx_T": ctx_T,
        "ctx_T_rev": ctx_T[:, ::-1].transpose(1, 0, 2, 3),
        "ctx_v": ctx_v,
        "lags": i["L0_xattn_ssm_kernel"],
        "skip": i["L0_xattn_D"],
        "gates": np.concatenate([i["g_xattn"], i["g_ffn"]]),
        "wr0": i["L0_ffn_w_gate"].reshape(KT, P, -1).transpose(1, 0, 2),
        "wr1": i["L1_ffn_w_router"].reshape(KT, P, -1).transpose(1, 0, 2),
        "bias1": i["L1_ffn_corr_bias"],
        "w0": _pack(np.concatenate([sgu0[:, :sh0], _flat(gu0[:, :, :m0])], axis=1),
                    np.concatenate([sgu0[:, sh0:], _flat(gu0[:, :, m0:])], axis=1),
                    np.concatenate([i["L0_ffn_w_sh_down"], i["L0_ffn_w_down"].reshape(-1, D)])),
        "w1": _pack(np.concatenate([np.pad(i["L1_ffn_sh_gate_w"], ((0, 0), (0, pad))), _flat(i["L1_ffn_gate_w"])], axis=1),
                    np.concatenate([np.pad(i["L1_ffn_sh_up_w"], ((0, 0), (0, pad))), _flat(i["L1_ffn_up_w"])], axis=1),
                    np.concatenate([np.pad(i["L1_ffn_sh_down_w"], ((0, pad), (0, 0))), i["L1_ffn_down_w"].reshape(-1, D)])),
    }


def kernel(**inputs):
    import concourse.bacc as _bacc
    from concourse.bass_utils import run_bass_kernel_spmd as _run

    nc = _bacc.Bacc("TRN2", target_bir_lowering=False, num_devices=1)
    arrays, args = {}, {}
    for name, v in _lay_out({k: np.asarray(v) for k, v in inputs.items()}).items():
        v = np.ascontiguousarray(v)
        arrays[f"in_{name}_dram"] = v
        args[name] = nc.dram_tensor(f"in_{name}_dram", v.shape, mybir.dt.from_np(v.dtype), kind="ExternalInput").ap()
    out = nc.dram_tensor("out_0_dram", (B, S, D), F32, kind="ExternalOutput").ap()
    build(nc, args, out)
    r = _run(nc, [arrays], core_ids=[0])
    return r.results[0]["out_0_dram"]
```

```python
from contextlib import ExitStack

import numpy as np

import concourse.bass as bass
from concourse import mybir
from concourse.alu_op_type import AluOpType as ALU

F32 = mybir.dt.float32
F32R = mybir.dt.float32r
BF16 = mybir.dt.bfloat16
U32 = mybir.dt.uint32
ACT = mybir.ActivationFunctionType
AX = mybir.AxisListType

P = 128
B, S, D = 8, 128, 256
T = B * S
KT = D // P
HALF = 512
NHALF = T // HALF
HB = HALF // S
A_HEADS, A_HD = 16, 8
C_HEADS, C_HD = 16, 16
TH = P // C_HD
HQ = 4
NQ = C_HEADS // HQ
TOEP = 4
EPS = 1e-5
RSQRT_MAGIC = 0x5F3759DF
MASK = -10000.0 * C_HD ** 0.5
LOWEST = -3.0e38

EXPERTS = [8, 32]
TOPK = [2, 6]
GROUPS, GSIZE, TOPG = 8, 4, 4
HID = [128, 176]
SHARED = [4, 3]
ROUTED = [E * M // P for E, M in zip(EXPERTS, HID)]
NT = [s + r for s, r in zip(SHARED, ROUTED)]
CHUNK = 16
GU = 2 * KT * P
WCOLS = GU + D


def build(nc, a, out):
    with ExitStack() as ctx:
        def sb(name, shape, dt=F32):
            return ctx.enter_context(nc.sbuf_tensor(name, shape, dt))

        def sem(name):
            return ctx.enter_context(nc.semaphore(name))

        X = sb("X", [P, B, D])
        xh = sb("xh", [P, B, D])
        xT_hi = sb("xT_hi", [P, KT, T], F32R)
        xT_lo = sb("xT_lo", [P, KT, T], F32R)
        ident = sb("ident", [P, P])
        ident_bf = sb("ident_bf", [P, P], BF16)
        gates = sb("gates", [P, 4])
        tgates = sb("tgates", [P, 4])
        bnst = sb("bnst", [P, B, 6])
        mv = sb("mv", [P, B, 2])
        rstd = sb("rstd", [P, B])
        nt1 = sb("nt1", [P, B])
        nt2 = sb("nt2", [P, B])
        magic = sb("magic", [P, B], U32)
        V = sb("V", [P, B, C_HEADS, C_HD + 1])
        KBD = sb("KBD", [P, B, KT, TH, S])
        cmask = sb("cmask", [P, HQ, S], BF16)
        lag_rows = sb("lag_rows", [A_HEADS, P + D])
        skip = sb("skip", [A_HEADS, 1])
        w_raw = sb("w_raw", [P, 2, WCOLS])
        bias1 = sb("bias1", [P, EXPERTS[1]])
        wr = [sb(f"wr{n}", [P, KT, EXPERTS[n]]) for n in range(2)]
        h_hi = [sb(f"h_hi{k}", [P, T], F32R) for k in range(2)]
        h_lo = [sb(f"h_lo{k}", [P, T], F32R) for k in range(2)]
        w_hi = [sb(f"w_hi{k}", [P, WCOLS], F32R) for k in range(2)]
        w_lo = [sb(f"w_lo{k}", [P, WCOLS], F32R) for k in range(2)]

        ARENA = 15 * 1024
        arena = sb("arena", [P, ARENA])
        at = [0]

        def take(*shape):
            n = int(np.prod(shape))
            v = arena[:, at[0]:at[0] + n]
            at[0] += n
            assert at[0] <= ARENA, at[0]
            if len(shape) == 1:
                return v
            names = "abcd"[:len(shape)]
            return v.rearrange(f"p ({' '.join(names)}) -> p {' '.join(names)}", **dict(zip(names, shape)))

        kT = take(KT, B, S)
        toep = [take(D) for _ in range(TOEP)]
        kv = [take(KT * B, A_HD, A_HD) for _ in range(2)]
        prod = [take(KT * B, A_HD, A_HD) for _ in range(2)]
        qT = take(KT, T)
        oA = take(KT * B, S)
        at[0] = 0
        sg = take(T)
        hh = take(T)
        cb = [take(T) for _ in range(2)]
        combT = take(T)
        yT = take(KT, T)
        xT = take(KT, T)
        router_words = at[0]
        rt = [take(B, EXPERTS[1]) for _ in range(8)]
        half_words = take(5, B, 16 + EXPERTS[1]).rearrange("p n b e -> p (n b e)").bitcast(BF16)
        counts = half_words.rearrange("p (n b e) -> p n b e", n=10, b=B)
        scan = [counts[:, n, :, :] for n in range(2)]
        ties, picked = counts[:, 2, :, 0:EXPERTS[1]], counts[:, 3, :, 0:EXPERTS[1]]
        top8 = take(B, 8)
        rs = [take(B) for _ in range(3)]
        comb = take(B, EXPERTS[1])
        gmask = take(B, GROUPS)
        at[0] = 0
        Sm = [take(HQ, S) for _ in range(2)]
        Pm = [[take(HQ, S) for _ in range(NQ)] for _ in range(2)]
        PTs = [take(HQ, S) for _ in range(2)]
        qc = [take(KT, S) for _ in range(2)]
        at[0] = router_words
        xr = [take(D) for _ in range(2)]
        mx = [take(HQ) for _ in range(2)]
        oC = take(C_HEADS, C_HD)
        rC = [take(C_HEADS) for _ in range(2)]

        psum = ctx.enter_context(nc.psum_tensor("psum", [P, 8, HALF], F32))
        bank = [psum[:, k, :] for k in range(8)]

        in_x = [sem(f"in_x{h}") for h in range(NHALF)]
        in_kT = [sem(f"in_kT{t}") for t in range(KT)]
        in_V, in_gates, in_small, in_kbd = (sem(n) for n in
            ("in_V", "in_gates", "in_small", "in_kbd"))
        in_lags, lags_ready, lags_out = sem("in_lags"), sem("lags_ready"), sem("lags_out")
        in_toep = [sem(f"in_toep{k}") for k in range(TOEP)]
        pool_const, pool_kbd0, pool_v1 = sem("pool_const"), sem("pool_kbd0"), sem("pool_v1")
        dve_step = sem("dve_step")
        act_gates = sem("act_gates")
        norm_ready = sem("norm_ready")
        xt_ready = sem("xt_ready")
        xt_out = sem("xt_out")
        xlo_ready = sem("xlo_ready")
        kv_begun = sem("kv_begun")
        kv_ready, conv_done, prod_ready, conv_out = (sem(n) for n in
            ("kv_ready", "conv_done", "prod_ready", "conv_out"))
        oT_ready = sem("oT_ready")
        x_new = sem("x_new")

        names = ("logits", "logits_kept", "router_in", "router_act", "comb_ready", "comb_T", "comb_copied",
                 "comb_out", "whi_gu", "whi_d", "first_lo", "wlo_gu", "wlo_d", "gu_done", "down_done", "silu_done",
                 "sc_done", "h_done", "hhi_done", "hlo_done", "y_bank", "y_copied", "yT_ready", "x_full")
        L = [{name: sem(f"{name}{n}") for name in names} for n in range(2)]
        w_in = [[sem(f"w_in{n}_{k}") for k in range(2)] for n in range(2)]
        c_in = [[sem(f"c_in{n}_{k}") for k in range(2)] for n in range(2)]
        (xr_ready, q_T, q_out, s_ready, mx_ready, sm_ready, exp_done, pt_ready, pt_out, pv_ready, o_out) = (
            sem(n) for n in ("xr_ready", "q_T", "q_out", "s_ready", "mx_ready", "sm_ready", "exp_done",
                             "pt_ready", "pt_out", "pv_ready", "o_out"))
        c_stats = sem("c_stats")
        comb_rest = sem("comb_rest")
        out_done = sem("out_done")

        comb_dram = [nc.dram_tensor("comb_rows0", (EXPERTS[0], T), F32, kind="Internal").ap(),
                     nc.dram_tensor("comb_rows1", (ROUTED[1] * P // CHUNK, T), F32, kind="Internal").ap()]

        lag_dram = nc.dram_tensor("lag_rows_dram", (A_HEADS, P + D), F32, kind="Internal").ap()

        def over(ap, *shape):
            return ap.unsqueeze(len(ap.shape)).broadcast_to([*ap.shape, shape[0]])

        XBANK = [[[5, 6], [7, 4]], [[2, 3], [5, 6]]]
        LOGITS = [5, 4]

        def out_bank(b):
            return bank[6 if isinstance(b, int) and b == B - 1 else 7]

        routed_pairs = [ROUTED[n] // 2 for n in range(2)]

        def turn(t, h):
            return 2 * h + t + 1 if isinstance(t, int) and t < 2 else 2 * t + (h + 1)

        def turn_before(t, h):
            return turn(t - 1, h) if isinstance(t, int) else 2 * t + (h - 1)

        block = ctx.enter_context(nc.Block())

        @block.sync
        def _(sp):
            sp.dma_start(lag_rows[:, P:], a["lags"]).then_inc(in_lags, 16)
            sp.dma_start(skip[:], a["skip"].unsqueeze(1)).then_inc(in_lags, 16)
            sp.dma_start(kT[:, 0], a["ctx_T_rev"][:, 0]).then_inc(in_kT[0], 16)
            sp.wait_ge(lags_ready, 2)
            sp.dma_start(lag_dram, lag_rows[:]).then_inc(lags_out, 16)
            sp.dma_start(kT[:, 1], a["ctx_T_rev"][:, 1]).then_inc(in_kT[1], 16)
            sp.wait_ge(lags_out, 16)
            toeplitz = bass.AP(lag_dram.tensor, lag_dram.offset + 1, [[1, P], [P + D, A_HEADS], [1, D]])

            def load_toep(h, k):
                sp.dma_start(toep[k], toeplitz[:, bass.ds(h, 1), :].rearrange("p o l -> p (o l)")).then_inc(in_toep[k], 16)

            for k in range(TOEP):
                load_toep(k, k)
            with sp.Fori(1, A_HEADS // TOEP) as i:
                for k in range(TOEP):
                    sp.wait_ge(conv_done, TOEP * i + (k + 1 - TOEP))
                    load_toep(TOEP * i + k, k)
            sp.wait_ge(pool_kbd0, 1)
            for h in range(TH):
                rows = slice(h * C_HD, (h + 1) * C_HD)
                for t in range(KT):
                    sp.dma_start(KBD[rows, :, t, h, :], a["ctx_T"][t, rows]).then_inc(in_kbd, 16)

            def expert_loads(n):
                q, R = L[n], ROUTED[n]

                def weights(t, k):
                    if isinstance(t, int) and t < 3:
                        sp.wait_ge(q["first_lo"], min(2 * t + 2, 5))
                    if not isinstance(t, int) or t >= 2:
                        sp.wait_ge(q["wlo_d"], t - 1)
                    sp.dma_start(w_raw[:, k, :], a[f"w{n}"][t + 2]).then_inc(w_in[n][k], 16)

                def combine(r, k):
                    if n == 0:
                        src = comb_dram[0][r].unsqueeze(0).broadcast_to([P, T])
                        sp.dma_start(cb[k], src).then_inc(c_in[n][k], 16)
                    else:
                        c = P // CHUNK
                        src = comb_dram[1][bass.ds(r * c, c), :].unsqueeze(1).broadcast_to([c, CHUNK, T])
                        sp.dma_start(cb[k], src).then_inc(c_in[n][k], 16)

                for t in range(3):
                    weights(t, t % 2)
                sp.wait_ge(q["comb_copied"], 2)
                if n == 0:
                    sp.dma_start(comb_dram[0], combT[0:EXPERTS[0], :]).then_inc(q["comb_out"], 16)
                else:
                    rep = HID[1] // CHUNK

                    def store(e0, e1, done):
                        sp.dma_start(comb_dram[1][e0 * rep:e1 * rep].rearrange("(e c) t -> e c t", c=rep),
                                     combT[e0:e1, :].unsqueeze(1).broadcast_to([e1 - e0, rep, T])).then_inc(done, 16)

                    store(0, 2, q["comb_out"])
                sp.wait_ge(q["comb_out"], 16)
                for k in range(2):
                    combine(k, k)
                for t in range(3, SHARED[n]):
                    weights(t, t % 2)

                def routed(i, k):
                    weights(2 * i + (SHARED[n] + k), (SHARED[n] + k) % 2)
                    if n == 1 and isinstance(i, int) and k == 0:
                        store(2, EXPERTS[1], comb_rest)
                        sp.wait_ge(comb_rest, 16)
                    sp.wait_ge(q["sc_done"], 4 * i + 2 * (k + 1))
                    combine(2 * i + (k + 2), k)

                for k in range(2):
                    routed(0, k)
                with sp.Fori(1, routed_pairs[n] - 1) as i:
                    for k in range(2):
                        routed(i, k)

            expert_loads(0)
            sp.wait_ge(L[0]["wlo_d"], NT[0] - 2)
            for k in range(2):
                sp.dma_start(w_raw[:, k, :], a["w1"][k]).then_inc(w_in[1][k], 16)
            expert_loads(1)
            for q in range(B // 2):
                sp.wait_ge(x_new, 8 + q + 1)
                sp.dma_start(out[2 * q:2 * q + 2].rearrange("b s d -> s b d"), X[:, 2 * q:2 * q + 2, :]).then_inc(out_done, 16)
            sp.wait_ge(out_done, 16 * (B // 2))

        @block.gpsimd
        def _(pool):
            def diagonal(m, n):
                pool.memset(m[:], 0.0).then_inc(pool_const, 1)
                pool.wait_ge(pool_const, n)
                pool.affine_select(out=m[:], in_=m[:], compare_op=ALU.not_equal, fill=1.0,
                                   base=0, pattern=[[-1, P]], channel_multiplier=1).then_inc(pool_const, 1)

            diagonal(ident, 1)

            kT3 = kT.rearrange("p t b s -> p (t b) s")

            def key_value(h, k, first):
                if not first:
                    pool.wait_ge(conv_done, h - 1)
                products(h, k, 0, KT).then_inc(kv_ready, 1)

            def products(h, k, t0, t1):
                n, src = (t1 - t0) * B, kT3[:, t0 * B:t1 * B, bass.ds(h * A_HD, A_HD)]
                return pool.tensor_tensor(kv[k][:, t0 * B:t1 * B], src.unsqueeze(3).broadcast_to([P, n, A_HD, A_HD]),
                                          src.unsqueeze(2).broadcast_to([P, n, A_HD, A_HD]), ALU.mult)

            pool.wait_ge(in_kT[0], 16)
            products(0, 0, 0, 1).then_inc(kv_begun, 1)
            pool.wait_ge(in_kT[1], 16)
            products(0, 0, 1, 2).then_inc(kv_ready, 1)
            key_value(1, 1, True)
            with pool.Fori(1, A_HEADS // 2) as i:
                for k in range(2):
                    key_value(2 * i + k, k, False)

            def first_low(n, tiles):
                q = L[n]
                for t in tiles:
                    k = t % 2
                    for cols, high in ((slice(0, GU), q["whi_gu"]), (slice(GU, WCOLS), q["whi_d"])):
                        if t == 2 and high is q["whi_d"]:
                            continue
                        pool.wait_ge(high, t + 1)
                        pool.tensor_tensor(w_lo[k][:, cols], w_raw[:, k, cols], w_hi[k][:, cols].bitcast(F32),
                                           ALU.subtract).then_inc(q["first_lo"], 1)

            diagonal(ident_bf, 3)
            pool.memset(cmask[:], 0.0).then_inc(pool_const, 1)
            pool.wait_ge(pool_const, 5)
            pool.affine_select(out=cmask[:], in_=cmask[:], compare_op=ALU.is_ge, fill=MASK,
                               base=0, pattern=[[0, HQ], [-1, S]], channel_multiplier=1).then_inc(pool_const, 1)
            pool.wait_ge(in_V, 16)
            pool.memset(V[:, :, :, C_HD:], 1.0).then_inc(pool_v1, 1)
            first_low(0, range(2))
            pool.memset(KBD[:], 0.0).then_inc(pool_kbd0, 1)
            first_low(0, [2])
            first_low(1, range(3))

        @block.scalar
        def _(act):
            for h in range(NHALF):
                act.dma_start(X[:, h * HB:(h + 1) * HB, :],
                              a["x"][h * HB:(h + 1) * HB].rearrange("b s d -> s b d")).then_inc(in_x[h], 16)
            act.dma_start(gates[:], a["gates"].unsqueeze(0).broadcast_to([P, 4])).then_inc(in_gates, 16)
            act.wait_ge(in_toep[1], 16)
            for k in range(2):
                act.dma_start(w_raw[:, k, :], a["w0"][k]).then_inc(w_in[0][k], 16)
            for n in range(2):
                act.dma_start(wr[n][:], a[f"wr{n}"]).then_inc(in_small, 16)
            act.dma_start(bias1[:], a["bias1"].unsqueeze(0).broadcast_to([P, EXPERTS[1]])).then_inc(in_small, 16)
            act.dma_start(V[:], a["ctx_v"]).then_inc(in_V, 16)
            act.wait_ge(in_gates, 16)
            act.activation(tgates[:], gates[:], ACT.Tanh).then_inc(act_gates, 1)

            for n, (h, t) in enumerate((h, t) for h in range(2) for t in range(KT)):
                act.wait_ge(xt_ready, n + 1)
                act.copy(qT[:, t, h * HALF:(h + 1) * HALF], bank[2 * t + h]).then_inc(xt_out, 1)

            def first_high(n):
                for t in range(2):
                    act.wait_ge(w_in[n][t], 16)
                    act.copy(w_hi[t][:, :GU], w_raw[:, t, :GU]).then_inc(L[n]["whi_gu"], 1)
                    act.copy(w_hi[t][:, GU:], w_raw[:, t, GU:]).then_inc(L[n]["whi_d"], 1)

            def x_high(n, transposed, h):
                for t in range(KT):
                    act.wait_ge(xt_ready, 4 * transposed + KT * h + t + 1)
                    act.copy(xT_hi[:, t, h * HALF:(h + 1) * HALF], bank[XBANK[n][h][t]]).then_inc(xt_out, 1)

            def experts(n, transposed):
                q, S0, N = L[n], SHARED[n], NT[n]

                def split_gu(t, k, landed=None):
                    act.wait_ge(w_in[n][k], 16 * (t // 2 + 1) if landed is None else landed)
                    act.wait_ge(q["gu_done"], turn(0, 1) if isinstance(t, int) and t == 2 else 2 * t - 2)
                    act.copy(w_hi[k][:, :GU], w_raw[:, k, :GU]).then_inc(q["whi_gu"], 1)

                def silu(t, h):
                    act.wait_ge(q["gu_done"], turn(t, h))
                    act.activation(sg[:, h * HALF:(h + 1) * HALF], bank[2 * h], ACT.Silu).then_inc(q["silu_done"], 1)

                def high(t, k, h):
                    cols = slice(h * HALF, (h + 1) * HALF)
                    act.wait_ge(q["h_done"], turn(t, h))
                    act.copy(h_hi[k][:, cols], hh[:, cols]).then_inc(q["hhi_done"], 1)

                def out_of_banks(h):
                    for t in range(KT):
                        act.wait_ge(q["y_bank"], KT * h + t + 1)
                        act.copy(yT[:, t, h * HALF:(h + 1) * HALF], bank[4 + 2 * t + h]).then_inc(q["y_copied"], 1)

                def step(t, k, landed=None, last=False, split=True):
                    if not last and split:
                        split_gu(t + 1, 1 - k, landed)
                    act.wait_ge(q["down_done"], t - 1)
                    act.copy(w_hi[k][:, GU:], w_raw[:, k, GU:]).then_inc(q["whi_d"], 1)
                    if last:
                        silu(t, 0)
                        high(t, k, 0)
                        silu(t, 1)
                        out_of_banks(0)
                        high(t, k, 1)
                        out_of_banks(1)
                        return
                    for h in range(NHALF):
                        silu(t, h)
                    for h in range(NHALF):
                        high(t, k, h)

                def x_whole(h):
                    for t in range(KT):
                        act.wait_ge(xlo_ready, 4 * (transposed - 1) + KT * h + t + 1)
                        act.copy(xT[:, t, h * HALF:(h + 1) * HALF], bank[XBANK[n][h][t]]).then_inc(q["x_full"], 1)

                x_whole(0)
                silu(0, 0)
                high(0, 0, 0)
                silu(1, 0)
                x_high(n, transposed, 1)
                x_whole(1)
                high(1, 1, 0)
                silu(0, 1)
                high(0, 0, 1)
                split_gu(2, 0)
                E = EXPERTS[n]
                if n == 0:
                    act.wait_ge(q["router_in"], 1)
                    act.activation(rt[1][:, :, 0:E], rt[0][:, :, 0:E], ACT.Exp).then_inc(q["router_act"], 1)
                else:
                    act.wait_ge(q["logits"], 1)
                    act.activation(rt[1][:, :, 0:E], bank[LOGITS[n]][:, 0:B * E].rearrange("p (b e) -> p b e", b=B),
                                   ACT.Sigmoid).then_inc(q["logits_kept"], 1)
                silu(1, 1)
                split_gu(3, 1)
                high(1, 1, 1)
                step(2, 0, split=False)
                for h in range(NHALF):
                    act.wait_ge(q["comb_T"], h + 1)
                    act.copy(combT[0:E, h * HALF:(h + 1) * HALF], bank[2 + h][0:E, :]).then_inc(q["comb_copied"], 1)
                for t in range(3, S0):
                    step(t, t % 2)
                with act.Fori(0, routed_pairs[n] - 1) as i:
                    for k in range(2):
                        step(2 * i + (S0 + k), (S0 + k) % 2, 16 * i + 16 * ((S0 + k + 1) // 2 + 1))
                step(N - 2, N % 2)
                step(N - 1, (N - 1) % 2, last=True)

            first_high(0)
            x_high(0, 1, 0)
            experts(0, 1)

            def queries(b, k):
                act.wait_ge(q_T, b + 1)
                act.copy(qc[k], bank[6][:, 0:D].rearrange("p (t s) -> p t s", t=KT)).then_inc(q_out, 1)

            def exponentials(b, k, j):
                act.wait_ge(sm_ready, NQ * b + (j + 1))
                act.activation(Pm[k][j], Sm[j % 2], ACT.Exp, scale=C_HD ** -0.5).then_inc(exp_done, 1)

            def attend(b, k, last=False, ahead=True):
                for j in range(NQ):
                    act.wait_ge(pt_ready, NQ * b + (j + 1))
                    act.copy(PTs[j % 2], bank[4 + j % 2].rearrange("p (h s) -> p h s", h=HQ)).then_inc(pt_out, 1)
                    if not last:
                        exponentials(b + 1, 1 - k, j)
                    elif j == 2:
                        x_high(1, 2, 0)
                    if j == 2 and ahead:
                        queries(b + 2, k)

            for b in range(2):
                queries(b, b)
            for j in range(NQ):
                exponentials(0, 0, j)
            attend(0, 0)
            with act.Fori(0, 2) as i:
                for k in range(2):
                    attend(2 * i + (1 + k), (1 + k) % 2)
            attend(5, 1)
            first_high(1)
            attend(6, 0, ahead=False)
            attend(7, 1, last=True, ahead=False)

            experts(1, 2)

        @block.vector
        def _(dve):
            class Chain:
                def __init__(self):
                    self.n = 0

                def add(self, ins):
                    ins.then_inc(dve_step, 1)
                    self.n += 1

                def wait(self):
                    dve.wait_ge(dve_step, self.n)

                def link(self, ins):
                    self.add(ins)
                    self.wait()

            chain = Chain()
            link = chain.link
            link(dve.memset(magic[:], RSQRT_MAGIC + 1))

            STEPS = 13

            def statistics_step(b0, b1, m):
                some = slice(b0, b1)
                y, v, t = rstd[:, some], nt2[:, some], nt1[:, some]
                chain.wait()
                if m == 0:
                    for b in range(b0, b1):
                        chain.add(dve.bn_aggr(mv[:, b, :], bnst[:, b, :]))
                elif m == 1:
                    chain.add(dve.tensor_scalar(v, mv[:, some, 1], EPS, None, ALU.add))
                elif m == 2:
                    chain.add(dve.tensor_scalar(t.bitcast(U32), v.bitcast(U32), 1, 0xFFFFFFFF,
                                                ALU.logical_shift_right, ALU.bitwise_xor))
                elif m == 3:
                    chain.add(dve.tensor_tensor(y.bitcast(U32), t.bitcast(U32), magic[:, some], ALU.add))
                elif m % 3 == 1:
                    chain.add(dve.scalar_tensor_tensor(out=t, in0=y, scalar=-0.5, in1=y, op0=ALU.mult, op1=ALU.mult))
                elif m % 3 == 2:
                    chain.add(dve.tensor_tensor(t, t, v, ALU.mult))
                else:
                    chain.add(dve.scalar_tensor_tensor(out=y, in0=t, scalar=1.5, in1=y, op0=ALU.add, op1=ALU.mult))

            def statistics(b0, b1, first=0, last=STEPS):
                for m in range(first, last):
                    statistics_step(b0, b1, m)

            def batch_statistics(b):
                chain.add(dve.bn_stats(bnst[:, b, :], X[:, b, :]))

            def norm_rows(b0, b1):
                chain.wait()
                for b in range(b0, b1):
                    dve.tensor_scalar(xh[:, b, :], X[:, b, :], mv[:, b, 0:1], rstd[:, b:b + 1],
                                      ALU.subtract, ALU.mult).then_inc(norm_ready, 1)

            q3 = qT.rearrange("p t (b s) -> p (t b) s", b=B)

            def weigh(h, k, first=False):
                dve.wait_ge(conv_done, h + 1)
                if not first:
                    dve.wait_ge(conv_out, h - 1)
                y = psum[:, 4 + 2 * k:6 + 2 * k, :].rearrange("p t (b j i) -> p (t b) j i", b=B, j=A_HD)
                q = q3[:, :, bass.ds(h * A_HD, A_HD)].unsqueeze(2).broadcast_to([P, KT * B, A_HD, A_HD])
                dve.tensor_tensor(prod[k], y, q, ALU.mult).then_inc(prod_ready, 1)

            def reduce(h, k):
                dve.wait_ge(prod_ready, h + 1)
                dve.tensor_reduce(oA[:, :, bass.ds(h * A_HD, A_HD)], prod[k], AX.X, ALU.add).then_inc(conv_out, 1)

            dve.memset(lag_rows[:, 0:P], 0.0).then_inc(lags_ready, 1)
            dve.wait_ge(in_lags, 32)
            dve.tensor_tensor(lag_rows[:, P:P + 1], lag_rows[:, P:P + 1], skip[:], ALU.add).then_inc(lags_ready, 1)
            for b in range(B):
                if b % HB == 0:
                    dve.wait_ge(in_x[b // HB], 16)
                batch_statistics(b)
                if b % HB == HB - 1:
                    statistics(b + 1 - HB, b + 1)
                    norm_rows(b + 1 - HB, b + 1)
            dve.wait_ge(xt_out, 4)
            for k in range(2):
                weigh(k, k, first=True)
            reduce(0, 0)
            with dve.Fori(0, A_HEADS // 2 - 1) as i:
                for k in range(2):
                    weigh(2 * i + (2 + k), k)
                    reduce(2 * i + (1 + k), 1 - k)
            reduce(A_HEADS - 1, 1)

            def add_pair(q, ready, gate, before):
                dve.wait_ge(ready, q + 1)
                rows = X[:, 2 * q:2 * q + 2, :].rearrange("p b d -> p (b d)")
                dve.scalar_tensor_tensor(out=rows, in0=bank[q], scalar=tgates[:, gate:gate + 1], in1=rows,
                                         op0=ALU.mult, op1=ALU.add).then_inc(x_new, 1)
                if before < 8:
                    dve.wait_ge(x_new, before + q + 1)
                    for b in (2 * q, 2 * q + 1):
                        batch_statistics(b)

            def top_begin(v, E, K):
                above, tied, first = picked[:, :, 0:E], ties[:, :, 0:E], scan[0][:, :, 16:16 + E]
                for b in range(B):
                    chain.add(dve.max(out=top8[:, b, :], in_=v[:, b, :]))
                chain.wait()
                kth = top8[:, :, K - 1:K].broadcast_to([P, B, E])
                chain.add(dve.tensor_tensor(above, v, kth, ALU.is_gt))
                chain.add(dve.tensor_tensor(tied, v, kth, ALU.is_equal))
                chain.wait()
                chain.add(dve.tensor_reduce(rs[0], above, AX.X, ALU.add))
                chain.add(dve.tensor_copy(first, tied))
                chain.wait()
                chain.add(dve.tensor_scalar(rs[1], rs[0], -1.0, float(K), ALU.mult, ALU.add))

            def top_end(E, sel):
                above, tied = picked[:, :, 0:E], ties[:, :, 0:E]
                cur, shift = 0, 1
                while shift < E:
                    link(dve.tensor_tensor(scan[1 - cur][:, :, 16:16 + E], scan[cur][:, :, 16:16 + E],
                                           scan[cur][:, :, 16 - shift:16 - shift + E], ALU.add))
                    cur, shift = 1 - cur, 2 * shift
                link(dve.tensor_tensor(scan[1 - cur][:, :, 16:16 + E], scan[cur][:, :, 16:16 + E], over(rs[1], E), ALU.is_le))
                link(dve.tensor_tensor(tied, tied, scan[1 - cur][:, :, 16:16 + E], ALU.mult))
                link(dve.tensor_tensor(sel, above, tied, ALU.add))

            def softmax_in(q, E):
                logits = bank[LOGITS[0]][:, 0:B * E].rearrange("p (b e) -> p b e", b=B)
                dve.wait_ge(q["logits"], 1)
                link(dve.tensor_reduce(rs[0], logits, AX.X, ALU.max))
                dve.tensor_tensor(rt[0][:, :, 0:E], logits, over(rs[0], E), ALU.subtract).then_inc(q["router_in"], 1)

            def choose0(q):
                E = EXPERTS[0]
                e, p = rt[1][:, :, 0:E], rt[2][:, :, 0:E]
                dve.wait_ge(q["router_act"], 1)
                link(dve.tensor_reduce(rs[0], e, AX.X, ALU.add))
                link(dve.reciprocal(rs[1], rs[0]))
                link(dve.tensor_tensor(p, e, over(rs[1], E), ALU.mult))
                top_begin(p, E, TOPK[0])

            def combine0(q):
                E = EXPERTS[0]
                p, sel, c = (rt[k][:, :, 0:E] for k in (2, 3, 4))
                top_end(E, sel)
                link(dve.tensor_tensor(c, p, sel, ALU.mult))
                link(dve.tensor_reduce(rs[0], c, AX.X, ALU.add))
                link(dve.reciprocal(rs[1], rs[0]))
                dve.tensor_tensor(comb[:, :, 0:E], c, over(rs[1], E), ALU.mult).then_inc(q["comb_ready"], 1)

            def group_scores(q):
                E = EXPERTS[1]
                score, sfc = rt[1], rt[2]
                dve.wait_ge(q["logits_kept"], 1)
                link(dve.tensor_tensor(sfc, score, bias1[:].unsqueeze(1).broadcast_to([P, B, E]), ALU.add))
                pair = sfc.rearrange("p b (x y) -> p (b x) y", y=2)
                hi2, lo2 = (rt[k].rearrange("p b e -> p (b e)")[:, 0:B * GROUPS * 2] for k in (4, 5))
                chain.add(dve.tensor_tensor(hi2, pair[:, :, 0], pair[:, :, 1], ALU.max))
                chain.add(dve.tensor_tensor(lo2, pair[:, :, 0], pair[:, :, 1], ALU.min))
                chain.wait()
                hi2, lo2 = (v.rearrange("p (g y) -> p g y", y=2) for v in (hi2, lo2))
                t1, t2, t3 = (rt[k].rearrange("p b e -> p (b e)")[:, B * GROUPS * 2:B * GROUPS * 3] for k in (4, 5, 6))
                gs = rt[6].rearrange("p b e -> p (b e)")[:, 0:B * GROUPS]
                chain.add(dve.tensor_tensor(t1, hi2[:, :, 0], hi2[:, :, 1], ALU.max))
                chain.add(dve.tensor_tensor(t2, hi2[:, :, 0], hi2[:, :, 1], ALU.min))
                chain.add(dve.tensor_tensor(t3, lo2[:, :, 0], lo2[:, :, 1], ALU.max))
                chain.wait()
                link(dve.tensor_tensor(t2, t2, t3, ALU.max))
                link(dve.tensor_tensor(gs, t1, t2, ALU.add))
                top_begin(gs.rearrange("p (b g) -> p b g", b=B), GROUPS, TOPG)

            def choose_groups():
                sfc = rt[2]
                top_end(GROUPS, gmask)
                fill = rt[4].rearrange("p b e -> p (b e)")[:, 0:B * GROUPS]
                gm = gmask.rearrange("p b g -> p (b g)")
                link(dve.tensor_scalar(fill, gm, 1.0, -LOWEST, ALU.subtract, ALU.mult))
                s4 = sfc.rearrange("p b (g e) -> p (b g) e", e=GSIZE)
                link(dve.tensor_tensor(s4, s4, over(gm, GSIZE), ALU.mult))
                link(dve.tensor_tensor(s4, s4, over(fill, GSIZE), ALU.add))

            def combine1(q):
                top_end(EXPERTS[1], rt[3])
                dve.tensor_tensor(comb, rt[1], rt[3], ALU.mult).then_inc(q["comb_ready"], 1)

            def low(n, transposed, h):
                for t in range(KT):
                    cols = slice(h * HALF, (h + 1) * HALF)
                    dve.wait_ge(xt_out, 4 * transposed + KT * h + t + 1)
                    dve.tensor_tensor(xT_lo[:, t, cols], bank[XBANK[n][h][t]], xT_hi[:, t, cols].bitcast(F32),
                                      ALU.subtract).then_inc(xlo_ready, 1)

            def hidden(n, t, h, r=None):
                q, cols = L[n], slice(h * HALF, (h + 1) * HALF)
                dve.wait_ge(q["silu_done"], turn(t, h))
                if not isinstance(t, int) or t > 0:
                    dve.wait_ge(q["hlo_done"], turn_before(t, h))
                if r is None:
                    dve.tensor_tensor(hh[:, cols], sg[:, cols], bank[2 * h + 1], ALU.mult).then_inc(q["h_done"], 1)
                else:
                    index, slot, landed = r
                    if h == 0:
                        dve.wait_ge(c_in[n][slot], landed)
                    dve.tensor_tensor(hh[:, cols], sg[:, cols], cb[slot][:, cols], ALU.mult).then_inc(q["sc_done"], 1)
                    dve.wait_ge(q["sc_done"], 2 * index + (h + 1))
                    dve.tensor_tensor(hh[:, cols], hh[:, cols], bank[2 * h + 1], ALU.mult).then_inc(q["h_done"], 1)

            def hidden_low(n, t, k, h):
                q, cols = L[n], slice(h * HALF, (h + 1) * HALF)
                dve.wait_ge(q["hhi_done"], turn(t, h))
                dve.tensor_tensor(h_lo[k][:, cols], hh[:, cols], h_hi[k][:, cols].bitcast(F32),
                                  ALU.subtract).then_inc(q["hlo_done"], 1)

            def experts(n, transposed):
                q, S0, N = L[n], SHARED[n], NT[n]

                def split_gu(t, k):
                    dve.wait_ge(q["whi_gu"], t + 1)
                    dve.tensor_tensor(w_lo[k][:, :GU], w_raw[:, k, :GU], w_hi[k][:, :GU].bitcast(F32),
                                      ALU.subtract).then_inc(q["wlo_gu"], 1)

                def split_down(t, k):
                    dve.wait_ge(q["whi_d"], t + 1)
                    dve.tensor_tensor(w_lo[k][:, GU:], w_raw[:, k, GU:], w_hi[k][:, GU:].bitcast(F32),
                                      ALU.subtract).then_inc(q["wlo_d"], 1)

                def step(t, k, r=None, last=False):
                    if not last:
                        split_gu(t + 1, 1 - k)
                    split_down(t, k)
                    if last:
                        for h in range(NHALF):
                            hidden(n, t, h, r)
                            hidden_low(n, t, k, h)
                        return
                    for h in range(NHALF):
                        hidden(n, t, h, r)
                    for h in range(NHALF):
                        hidden_low(n, t, k, h)

                hidden_low(n, 0, 0, 0)
                low(n, transposed, 1)
                hidden(n, 1, 0)
                hidden_low(n, 1, 1, 0)
                hidden(n, 0, 1)
                hidden_low(n, 0, 0, 1)
                if n == 0:
                    softmax_in(q, EXPERTS[0])
                else:
                    group_scores(q)
                hidden(n, 1, 1)
                split_gu(3, 1)
                if n == 1:
                    choose_groups()
                hidden_low(n, 1, 1, 1)
                split_down(2, 0)
                if n == 0:
                    choose0(q)
                else:
                    top_begin(rt[2], EXPERTS[1], TOPK[1])
                hidden(n, 2, 0)
                (combine0 if n == 0 else combine1)(q)
                hidden(n, 2, 1)
                for h in range(NHALF):
                    hidden_low(n, 2, 0, h)
                for t in range(3, S0):
                    step(t, t % 2)
                with dve.Fori(0, routed_pairs[n] - 1) as i:
                    for k in range(2):
                        step(2 * i + (S0 + k), (S0 + k) % 2, (2 * i + k, k, 16 * i + 16))
                for k in range(2):
                    step(N - 2 + k, (N + k) % 2, (ROUTED[n] - 2 + k, k, 16 * routed_pairs[n]), last=k == 1)

            def clear_counts():
                for c in counts[:, 0, :, 0:16], counts[:, 1, :, 0:16]:
                    chain.add(dve.memset(c, 0.0))

            clear_counts()
            dve.wait_ge(act_gates, 1)
            add_pair(0, oT_ready, 0, 0)
            add_pair(1, oT_ready, 0, 0)
            statistics(0, HB)
            norm_rows(0, HB)
            add_pair(2, oT_ready, 0, 0)
            low(0, 1, 0)
            add_pair(3, oT_ready, 0, 0)
            statistics(HB, B, 0, 9)
            hidden(0, 0, 0)
            statistics(HB, B, 9)
            norm_rows(HB, B)
            experts(0, 1)

            def normed(b, k):
                dve.tensor_scalar(xr[k], X[:, bass.ds(b, 1), :].rearrange("p o d -> p (o d)"), mv[:, bass.ds(b, 1), 0:1].rearrange("p o c -> p (o c)"), rstd[:, bass.ds(b, 1)],
                                  ALU.subtract, ALU.mult).then_inc(xr_ready, 1)

            def less_maximum(b, j, first=False):
                scores = bank[j].rearrange("p (h s) -> p h s", h=HQ)
                dve.wait_ge(s_ready, NQ * b + (j + 1))
                dve.tensor_reduce(mx[j % 2], scores, AX.X, ALU.max).then_inc(mx_ready, 1)
                dve.wait_ge(mx_ready, NQ * b + (j + 1))
                if not (first and j < 2):
                    dve.wait_ge(exp_done, NQ * b + (j - 1))
                dve.tensor_tensor(Sm[j % 2], scores, over(mx[j % 2], S), ALU.subtract).then_inc(sm_ready, 1)

            def add_heads(b):
                o = out_bank(b)[:, 0:C_HEADS * (C_HD + 1)].rearrange("p (h c) -> p h c", h=C_HEADS)
                dve.wait_ge(pv_ready, b + 1)
                dve.reciprocal(rC[0], o[:, :, C_HD]).then_inc(o_out, 1)
                dve.wait_ge(o_out, 4 * b + 1)
                dve.tensor_scalar(rC[1], rC[0], tgates[:, 1:2], None, ALU.mult).then_inc(o_out, 1)
                dve.wait_ge(o_out, 4 * b + 2)
                dve.tensor_tensor(oC, o[:, :, 0:C_HD], over(rC[1], C_HD), ALU.mult).then_inc(o_out, 1)
                dve.wait_ge(o_out, 4 * b + 3)
                xb = X[:, bass.ds(b, 1), :].rearrange("p o d -> p (o d)")
                dve.tensor_tensor(xb, xb, oC.rearrange("p h c -> p (h c)"), ALU.add).then_inc(o_out, 1)
                dve.wait_ge(o_out, 4 * b + 4)
                dve.bn_stats(bnst[:, bass.ds(b, 1), :].rearrange("p o c -> p (o c)"), xb).then_inc(c_stats, 1)

            y0 = L[0]["yT_ready"]
            add_pair(0, y0, 2, 4)
            statistics(0, 2)
            chain.wait()
            for b in range(2):
                normed(b, b)
            for q in range(1, B // 2):
                add_pair(q, y0, 2, 4)
                less_maximum(0, q - 1, first=True)
            statistics(2, B, 0, 3)
            less_maximum(0, NQ - 1, first=True)
            statistics(2, B, 3, 6)
            less_maximum(1, 0)
            statistics(2, B, 6, 9)
            less_maximum(1, 1)
            statistics(2, B, 9)
            chain.wait()
            dve.wait_ge(q_out, 1)
            normed(2, 0)
            less_maximum(1, 2)
            less_maximum(1, 3)

            def attend(b, k, first=False, last=False, ahead=True, steps=()):
                if ahead:
                    dve.wait_ge(q_out, b + 1)
                    normed(b + 2, k)
                for j in range(NQ):
                    if not last:
                        less_maximum(b + 1, j)
                    if j == 0 and not first:
                        add_heads(b - 1)
                    for m in steps[j * len(steps) // NQ:(j + 1) * len(steps) // NQ]:
                        statistics_step(0, HB, m)

            with dve.Fori(0, 2) as i:
                for k in range(2):
                    attend(2 * i + (1 + k), (1 + k) % 2)
            dve.wait_ge(c_stats, HB)
            attend(5, 1, steps=range(7))
            attend(6, 0, ahead=False, steps=range(7, STEPS))
            norm_rows(0, HB)
            attend(7, 1, last=True, ahead=False)
            clear_counts()
            low(1, 2, 0)
            add_heads(7)
            dve.wait_ge(c_stats, B)
            statistics(HB, B, 0, 5)
            hidden(1, 0, 0)
            statistics(HB, B, 5)
            norm_rows(HB, B)
            experts(1, 2)
            for q in range(B // 2):
                add_pair(q, L[1]["yT_ready"], 3, 8)

        @block.tensor
        def _(pe):
            def transpose_norm(n, h, banks):
                for t in range(KT):
                    for b in range(h * HB, (h + 1) * HB):
                        pe.wait_ge(norm_ready, B * n + b + 1)
                        c = (b - h * HB) * S
                        mm = pe.transpose(bank[banks[t]][:, c:c + S], xh[:, b, t * P:(t + 1) * P], ident[:])
                    mm.then_inc(xt_ready, 1)

            def keep_clock(n, free, operand):
                for _ in range(n):
                    pe.matmul(bank[free], ident[:], operand, start=True, stop=True)

            def convolve(h, slot, landed, first=False):
                k = slot % 2
                if isinstance(h, int) and h == 0:
                    pe.wait_ge(kv_begun, 1)
                else:
                    pe.wait_ge(kv_ready, h + 1)
                pe.wait_ge(in_toep[slot], landed)
                if not first:
                    pe.wait_ge(prod_ready, h - 1)
                near, far = toep[slot][:, 0:P], toep[slot][:, P:D]
                kv0, kv1 = (kv[k][:, t * B:(t + 1) * B].rearrange("p b j i -> p (b j i)") for t in range(KT))
                pe.matmul(bank[4 + 2 * k], near, kv0, start=True, stop=True)
                pe.matmul(bank[5 + 2 * k], far, kv0, start=True, stop=False)
                if isinstance(h, int) and h == 0:
                    pe.wait_ge(kv_ready, 1)
                pe.matmul(bank[5 + 2 * k], near, kv1, start=False, stop=True).then_inc(conv_done, 1)

            convolve(0, 0, 16, first=True)
            pe.wait_ge(pool_const, 2)
            for h in range(NHALF):
                transpose_norm(0, h, [h, 2 + h])
            convolve(1, 1, 16, first=True)
            for k in range(2, TOEP):
                convolve(k, k, 16)
            with pe.Fori(1, A_HEADS // TOEP) as i:
                for k in range(TOEP):
                    convolve(TOEP * i + k, k, 16 * i + 16)
            spare = kv[0][:, 0:B].rearrange("p b j i -> p (b j i)")
            keep_clock(4, 3, spare)
            pe.wait_ge(conv_out, A_HEADS)
            for q in range(B // 2):
                for b in (2 * q, 2 * q + 1):
                    for t in range(KT):
                        c = (b % 2) * D + t * P
                        mm = pe.transpose(bank[q][:, c:c + P], oA[:, t * B + b, :], ident[:])
                mm.then_inc(oT_ready, 1)

            def experts(n, norm, transposed):
                q, S0, N, E = L[n], SHARED[n], NT[n], EXPERTS[n]

                def gate_up_half(t, k, h):
                    x = slice(h * HALF, (h + 1) * HALF)
                    for g in range(2):
                        m = 0
                        for c in range(KT):
                            w = slice((g * KT + c) * P, (g * KT + c + 1) * P)
                            for wp, xp in ((w_hi[k], xT_hi), (w_hi[k], xT_lo), (w_lo[k], xT_hi)):
                                mm = pe.matmul(bank[2 * h + g], wp[:, w], xp[:, c, x], start=m == 0, stop=m == 3 * KT - 1)
                                m += 1
                    mm.then_inc(q["gu_done"], 1)

                def left(t, h):
                    pe.wait_ge(q["silu_done"], turn_before(t, h))
                    pe.wait_ge(q["h_done"], turn_before(t, h))

                def gate_up(t, k):
                    pe.wait_ge(q["wlo_gu"], t - 2)
                    for h in range(NHALF):
                        left(t, h)
                        gate_up_half(t, k, h)

                def down_half(t, k, h, first=False, last=False):
                    pe.wait_ge(q["hlo_done"], turn(t, h))
                    x = slice(h * HALF, (h + 1) * HALF)
                    for c in range(KT):
                        w = slice(GU + c * P, GU + (c + 1) * P)
                        for m, (wp, hp) in enumerate(((w_hi[k], h_hi[k]), (w_hi[k], h_lo[k]), (w_lo[k], h_hi[k]))):
                            mm = pe.matmul(bank[4 + 2 * c + h], wp[:, w], hp[:, x], start=first and m == 0,
                                           stop=last and m == 2, skip_group_check=True)
                        if last:
                            mm.then_inc(q["y_bank"], 1)
                    return mm

                def down(t, k, first=False):
                    if isinstance(t, int) and t < 2:
                        pe.wait_ge(q["first_lo"], 2 * t + 2)
                    else:
                        pe.wait_ge(q["wlo_d"], t - 1)
                    for h in range(NHALF):
                        mm = down_half(t, k, h, first)
                    mm.then_inc(q["down_done"], 1)

                def logits(b0, b1):
                    pe.wait_ge(q["x_full"], KT * (b0 // HB + 1))
                    for b in range(b0, b1):
                        for c in range(KT):
                            mm = pe.matmul(bank[LOGITS[n]][:, b * E:(b + 1) * E], xT[:, c, b * S:(b + 1) * S], wr[n][:, c, :],
                                           start=c == 0, stop=c == KT - 1)
                    return mm

                pe.wait_ge(q["first_lo"], 1)
                pe.wait_ge(xlo_ready, 4 * (transposed - 1) + KT)
                gate_up_half(0, 0, 0)
                pe.wait_ge(in_small, 48)
                logits(0, HB // 2)
                pe.wait_ge(q["first_lo"], 3)
                left(1, 0)
                gate_up_half(1, 1, 0)
                transpose_norm(norm, 1, XBANK[n][1])
                logits(HB // 2, HB)
                pe.wait_ge(xlo_ready, 4 * transposed)
                gate_up_half(0, 0, 1)
                logits(HB, B).then_inc(q["logits"], 1)
                left(1, 1)
                gate_up_half(1, 1, 1)
                pe.wait_ge(q["router_in" if n == 0 else "logits_kept"], 1)
                down(0, 0, first=True)
                pe.wait_ge(q["first_lo"], 5)
                for h in range(NHALF):
                    left(2, h)
                    gate_up_half(2, 0, h)
                down(1, 1)
                pe.wait_ge(q["wlo_gu"], 1)
                left(3, 0)
                gate_up_half(3, 1, 0)
                left(3, 1)
                pe.wait_ge(q["comb_ready"], 1)
                for h in range(NHALF):
                    for b in range(h * HB, (h + 1) * HB):
                        c = (b - h * HB) * S
                        mm = pe.transpose(bank[2 + h][0:E, c:c + S], comb[:, b, 0:E], ident[:])
                    mm.then_inc(q["comb_T"], 1)
                pe.wait_ge(q["comb_copied"], 2)
                gate_up_half(3, 1, 1)
                down(2, 0)
                pairs = (N - 6) // 2
                with pe.Fori(0, pairs) as i:
                    for k in range(2):
                        gate_up(2 * i + (4 + k), k)
                        down(2 * i + (3 + k), 1 - k)
                for t in range(4 + 2 * pairs, N - 2):
                    gate_up(t, t % 2)
                    down(t - 1, (t - 1) % 2)

                def to_rows(h):
                    pe.wait_ge(q["y_copied"], KT * (h + 1))
                    for p in range(h * HB // 2, (h + 1) * HB // 2):
                        for b in (2 * p, 2 * p + 1):
                            for t in range(KT):
                                c = (b % 2) * D + t * P
                                mm = pe.transpose(bank[p][:, c:c + P], yT[:, t, b * S:(b + 1) * S], ident[:])
                        mm.then_inc(q["yT_ready"], 1)

                gate_up(N - 2, N % 2)
                down(N - 3, (N - 3) % 2)
                pe.wait_ge(q["wlo_gu"], N - 3)
                for h in range(NHALF):
                    left(N - 1, h)
                    gate_up_half(N - 1, (N - 1) % 2, h)
                    if h == 0:
                        pe.wait_ge(q["wlo_d"], N - 3)
                        down_half(N - 2, N % 2, 0)
                pe.wait_ge(q["wlo_d"], N - 2)
                down_half(N - 1, (N - 1) % 2, 0, last=True)
                down_half(N - 2, N % 2, 1)
                to_rows(0)
                down_half(N - 1, (N - 1) % 2, 1, last=True)
                to_rows(1)

            keep_clock(6, 7, spare)
            transpose_norm(1, 0, XBANK[0][0])
            experts(0, 1, 1)

            def queries(b, k):
                pe.wait_ge(xr_ready, b + 1)
                if not isinstance(b, int) or b > 0:
                    pe.wait_ge(q_out, b)
                for t in range(KT):
                    mm = pe.transpose(bank[6][:, t * S:(t + 1) * S], xr[k][:, t * P:(t + 1) * P], ident[:])
                mm.then_inc(q_T, 1)

            def scores(b, k, j, first=False):
                if j == 0:
                    pe.wait_ge(q_out, b + 1)
                if first:
                    pe.wait_ge(x_new, 4 + j + 1)
                else:
                    pe.wait_ge(sm_ready, NQ * b + (j + 1 - NQ))
                t, h = j // (NQ // KT), HQ * (j % (NQ // KT))
                pe.matmul(bank[j], ident_bf[:], cmask[:].rearrange("p h s -> p (h s)"), start=True, stop=False)
                pe.matmul(bank[j], qc[k][:, t, :], KBD[:, bass.ds(b, 1), t, h:h + HQ, :].rearrange("p o h s -> p (o h s)"),
                          start=False, stop=True).then_inc(s_ready, 1)

            def values(b, j, wait_out=True):
                pe.wait_ge(pt_out, NQ * b + (j + 1))
                if j == 0 and wait_out:
                    pe.wait_ge(o_out, 4 * b - 1)
                for h in range(HQ):
                    head = HQ * j + h
                    c = head * (C_HD + 1)
                    mm = pe.matmul(out_bank(b)[:, c:c + C_HD + 1], PTs[j % 2][:, h, :],
                                   V[:, bass.ds(b, 1), head, :].rearrange("p o c -> p (o c)"), start=True, stop=True)
                if j == NQ - 1:
                    mm.then_inc(pv_ready, 1)

            def attend(b, k, first=False, last=False, ahead=True):
                for j in range(NQ):
                    if not last:
                        scores(b + 1, 1 - k, j)
                    pe.wait_ge(exp_done, NQ * b + (j + 1))
                    if not (first and j < 2):
                        pe.wait_ge(pt_out, NQ * b + (j - 1))
                    for h in range(HQ):
                        mm = pe.transpose(bank[4 + j % 2][:, h * S:(h + 1) * S], Pm[k][j][:, h, :], ident[:])
                    mm.then_inc(pt_ready, 1)
                    if j == 2 and ahead:
                        queries(b + 2, k)
                    if j > 0:
                        values(b, j - 1, wait_out=not first and not last)
                    elif not first:
                        values(b - 1, NQ - 1)
                    if last and j == 1:
                        transpose_norm(2, 0, XBANK[1][0])

            pe.wait_ge(pool_v1, 1)
            pe.wait_ge(pool_const, 6)
            pe.wait_ge(in_kbd, 16 * TH * KT)
            busy = KBD[:, 0, 0, 0:HQ, :].rearrange("p h s -> p (h s)")
            keep_clock(1, 7, busy)
            for b in range(2):
                queries(b, b)
            for j in range(NQ):
                scores(0, 0, j, first=True)
            attend(0, 0, first=True)
            with pe.Fori(0, 2) as i:
                for k in range(2):
                    attend(2 * i + (1 + k), (1 + k) % 2)
            attend(5, 1)
            attend(6, 0, ahead=False)
            attend(7, 1, last=True, ahead=False)
            keep_clock(1, 0, busy)
            values(7, NQ - 1)

            experts(1, 2, 2)


def _pack(gate, up, down):
    n = gate.shape[1] // P
    g, u = (w.reshape(KT, P, n, P).transpose(2, 1, 0, 3).reshape(n, P, KT * P) for w in (gate, up))
    return np.concatenate([g, u, down.reshape(n, P, D)], axis=2)


def _flat(w):
    return w.transpose(1, 0, 2).reshape(D, -1)


def _lay_out(i):
    pad = SHARED[1] * P - i["L1_ffn_sh_gate_w"].shape[1]
    ctx_T = np.ascontiguousarray(i["ctx_2048"].transpose(2, 0, 1)).reshape(KT, P, B, S)
    gu0, sgu0 = i["L0_ffn_w_gate_up"], i["L0_ffn_w_sh_gate_up"]
    m0, sh0 = HID[0], SHARED[0] * P
    ctx_v = np.ones((S, B, C_HEADS, C_HD + 1), np.float32)
    ctx_v[..., :C_HD] = i["ctx_2048"].transpose(1, 0, 2).reshape(S, B, C_HEADS, C_HD)
    return {
        "x": i["x"],
        "ctx_T": ctx_T,
        "ctx_T_rev": ctx_T[:, ::-1].transpose(1, 0, 2, 3),
        "ctx_v": ctx_v,
        "lags": i["L0_xattn_ssm_kernel"],
        "skip": i["L0_xattn_D"],
        "gates": np.concatenate([i["g_xattn"], i["g_ffn"]]),
        "wr0": i["L0_ffn_w_gate"].reshape(KT, P, -1).transpose(1, 0, 2),
        "wr1": i["L1_ffn_w_router"].reshape(KT, P, -1).transpose(1, 0, 2),
        "bias1": i["L1_ffn_corr_bias"],
        "w0": _pack(np.concatenate([sgu0[:, :sh0], _flat(gu0[:, :, :m0])], axis=1),
                    np.concatenate([sgu0[:, sh0:], _flat(gu0[:, :, m0:])], axis=1),
                    np.concatenate([i["L0_ffn_w_sh_down"], i["L0_ffn_w_down"].reshape(-1, D)])),
        "w1": _pack(np.concatenate([np.pad(i["L1_ffn_sh_gate_w"], ((0, 0), (0, pad))), _flat(i["L1_ffn_gate_w"])], axis=1),
                    np.concatenate([np.pad(i["L1_ffn_sh_up_w"], ((0, 0), (0, pad))), _flat(i["L1_ffn_up_w"])], axis=1),
                    np.concatenate([np.pad(i["L1_ffn_sh_down_w"], ((0, pad), (0, 0))), i["L1_ffn_down_w"].reshape(-1, D)])),
    }


def kernel(**inputs):
    import concourse.bacc as _bacc
    from concourse.bass_utils import run_bass_kernel_spmd as _run

    nc = _bacc.Bacc("TRN2", target_bir_lowering=False, num_devices=1)
    arrays, args = {}, {}
    for name, v in _lay_out({k: np.asarray(v) for k, v in inputs.items()}).items():
        v = np.ascontiguousarray(v)
        arrays[f"in_{name}_dram"] = v
        args[name] = nc.dram_tensor(f"in_{name}_dram", v.shape, mybir.dt.from_np(v.dtype), kind="ExternalInput").ap()
    out = nc.dram_tensor("out_0_dram", (B, S, D), F32, kind="ExternalOutput").ap()
    build(nc, args, out)
    r = _run(nc, [arrays], core_ids=[0])
    return r.results[0]["out_0_dram"]
```
